# Optimizing a Trainium2 kernel written in Bass

```python
import numpy as np
import jax
import jax.numpy as jnp

def _softmax(x, axis=-1):
    return jax.nn.softmax(x, axis=axis)
def _gelu(x):
    return jax.nn.gelu(x, approximate=True)
def _silu(x):
    return jax.nn.silu(x)
def _sigmoid(x):
    return jax.nn.sigmoid(x)
def _layernorm(x, axis=-1, eps=1e-5):
    m = jnp.mean(x, axis=axis, keepdims=True)
    v = jnp.var(x, axis=axis, keepdims=True)
    return (x - m) / jnp.sqrt(v + eps)
def _scatter_add(tgt, idx, src, axis=0):
    return tgt.at[idx].add(src)
def _segment_sum(src, seg, n):
    return jax.ops.segment_sum(src, seg, n)

kernel_name = 'mk_metaformer_d1_conv_nchw256_f18715'

def setup_inputs(seed: int = 0):
    np.random.seed(seed)
    _w = jnp.asarray
    def _rec_inputs():
        import jax
        import jax.numpy as jnp
        _gk = jax.random.key(seed)
        x = -0.000929 + 1 * jax.random.normal(jax.random.fold_in(_gk, 1), (1, 256, 64, 64), jnp.float32)
        return x
    x = _rec_inputs()
    def _L0_conv_setup():
        import jax, jax.numpy as jnp
        import numpy as np
        N_FEAT = 256
        NUM_HEADS = 8
        EPS = 1e-12

        def _l2norm(t):
            n = jnp.linalg.norm(t, axis=-1, keepdims=True)
            return t / jnp.maximum(n, EPS)
        key = jax.random.key(seed)
        k1, k2, k3 = jax.random.split(key, 3)
        b, c, h, w = (1, N_FEAT, 64, 64)
        x = jax.random.normal(k1, (b, c, h, w), dtype=jnp.float32)
        w_qkv = jax.random.normal(k2, (3 * c, c), dtype=jnp.float32) * (1.0 / np.sqrt(c))
        w_proj = jax.random.normal(k3, (c, c), dtype=jnp.float32) * (1.0 / np.sqrt(c))
        temperature = jnp.ones((NUM_HEADS, 1, 1), dtype=jnp.float32)
        return {'x': x, 'w_qkv': w_qkv, 'w_proj': w_proj, 'temperature': temperature}
    _L0_conv_all = _L0_conv_setup()
    _L0_conv_in = {k: v for k, v in _L0_conv_all.items() if k in ('w_qkv', 'w_proj', 'temperature', )}
    del _L0_conv_all

    def _L0_ffn_setup():
        import jax, jax.numpy as jnp
        import numpy as np
        N_EXPERTS = 8
        TOP_K = 2
        key = jax.random.key(seed)
        ks = jax.random.split(key, 5)
        B, T, C, E, H = (8, 2048, 256, 8, 682)
        scale = 1.0 / np.sqrt(C)
        return {'x': jax.random.normal(ks[0], (B, T, C), dtype=jnp.float32), 'router_w': jax.random.normal(ks[1], (E, C), dtype=jnp.float32) * scale, 'w1': jax.random.normal(ks[2], (E, H, C), dtype=jnp.float32) * scale, 'w2': jax.random.normal(ks[3], (E, C, H), dtype=jnp.float32) * (1.0 / np.sqrt(H)), 'w3': jax.random.normal(ks[4], (E, H, C), dtype=jnp.float32) * scale}
    _L0_ffn_all = _L0_ffn_setup()
    _L0_ffn_in = {k: v for k, v in _L0_ffn_all.items() if k in ('router_w', 'w1', 'w2', 'w3', )}
    del _L0_ffn_all

    return {
        "x": x,
        "L0_conv_w_qkv": _L0_conv_in["w_qkv"],
        "L0_conv_w_proj": _L0_conv_in["w_proj"],
        "L0_conv_temperature": _L0_conv_in["temperature"],
        "L0_ffn_router_w": _L0_ffn_in["router_w"],
        "L0_ffn_w1": _L0_ffn_in["w1"],
        "L0_ffn_w2": _L0_ffn_in["w2"],
        "L0_ffn_w3": _L0_ffn_in["w3"],
    }

def reference(x, L0_conv_w_qkv, L0_conv_w_proj, L0_conv_temperature, L0_ffn_router_w, L0_ffn_w1, L0_ffn_w2, L0_ffn_w3):
    import jax
    import jax.numpy as jnp
    def _L0_conv_ref(x, w_qkv, w_proj, temperature):
        import jax, jax.numpy as jnp
        import numpy as np
        N_FEAT = 256
        NUM_HEADS = 8
        EPS = 1e-12

        def _l2norm(t):
            n = jnp.linalg.norm(t, axis=-1, keepdims=True)
            return t / jnp.maximum(n, EPS)
        b, c, h, w = x.shape
        heads = temperature.shape[0]
        d = c // heads
        hw = h * w
        xf = x.reshape(b, c, hw)
        qkv = jnp.einsum('oc,bcs->bos', w_qkv, xf)
        qkv = qkv.reshape(b, 3, heads, d, hw)
        q, k, v = (qkv[:, 0], qkv[:, 1], qkv[:, 2])
        q = jnp.swapaxes(q, -2, -1)
        k = jnp.swapaxes(k, -2, -1)
        v = jnp.swapaxes(v, -2, -1)
        q = _l2norm(q)
        k = _l2norm(k)
        attn = jnp.einsum('bhsd,bhtd->bhst', q, k) * temperature[None]
        attn = jax.nn.softmax(attn, axis=-1)
        out = jnp.einsum('bhst,bhtd->bhsd', attn, v)
        out = out.transpose(0, 2, 1, 3).reshape(b, c, h, w)
        out = jnp.einsum('oc,bchw->bohw', w_proj, out)
        return out

    def _L0_ffn_ref(x, router_w, w1, w2, w3):
        import jax, jax.numpy as jnp
        import numpy as np
        N_EXPERTS = 8
        TOP_K = 2
        B, T, C = x.shape
        flat = x.reshape(-1, C)
        logits = flat @ router_w.T
        probs = jax.nn.softmax(logits, axis=-1)
        topk_probs, topk_idx = jax.lax.top_k(probs, TOP_K)
        topk_probs = topk_probs / (jnp.sum(topk_probs, axis=-1, keepdims=True) + 1e-09)
        onehot = jax.nn.one_hot(topk_idx, N_EXPERTS, dtype=flat.dtype)
        gates = jnp.einsum('nk,nke->ne', topk_probs, onehot)
        h1 = jnp.einsum('nc,ehc->neh', flat, w1)
        h3 = jnp.einsum('nc,ehc->neh', flat, w3)
        h = jax.nn.silu(h1) * h3
        y = jnp.einsum('neh,ech->nec', h, w2)
        out = jnp.einsum('ne,nec->nc', gates, y)
        return out.reshape(B, T, C)

    def _gn(v, G=32, eps=1e-5):
        B_, C_, H_, W_ = v.shape
        g = v.reshape(B_, G, C_ // G, H_, W_)
        m = jnp.mean(g, axis=(2, 3, 4), keepdims=True)
        s = jnp.var(g, axis=(2, 3, 4), keepdims=True)
        return ((g - m) / jnp.sqrt(s + eps)).reshape(v.shape)

    def _ln_c(v, eps=1e-6):
        m = jnp.mean(v, axis=1, keepdims=True)
        s = jnp.var(v, axis=1, keepdims=True)
        return (v - m) / jnp.sqrt(s + eps)

    def _ln_t(v, eps=1e-5):
        m = jnp.mean(v, axis=-1, keepdims=True)
        s = jnp.var(v, axis=-1, keepdims=True)
        return (v - m) / jnp.sqrt(s + eps)

    def _to_tokens(v):
        B_, C_, H_, W_ = v.shape
        return v.reshape(B_, C_, H_ * W_).transpose(0, 2, 1)
    def _from_tokens(t, like):
        B_, C_, H_, W_ = like.shape
        return t.transpose(0, 2, 1).reshape(B_, C_, H_, W_)

    x = x + _L0_conv_ref(_ln_c(x), L0_conv_w_qkv, L0_conv_w_proj, L0_conv_temperature)
    t = _to_tokens(x)
    t = t + _L0_ffn_ref(_ln_t(t), L0_ffn_router_w, L0_ffn_w1, L0_ffn_w2, L0_ffn_w3)
    x = _from_tokens(t, x)
    return x


_drawn_inputs = setup_inputs


def setup_inputs(seed=0):
    import zlib

    import numpy as np

    out = dict(_drawn_inputs(seed))
    spreads = {'L0_conv_temperature': (1.0, 0.2)}
    factors = {}
    for name, (base, spread) in spreads.items():
        noise = np.random.default_rng([zlib.crc32(name.encode()), seed]).standard_normal(out[name].shape)
        drawn = base * np.exp(spread * noise) if base else spread * noise
        out[name] = jnp.asarray(drawn.astype(out[name].dtype))
    for name, factor in factors.items():
        out[name] = (out[name] * factor).astype(out[name].dtype)
    return out
```

```python
from contextlib import ExitStack

import concourse.bass as bass
from concourse import mybir

F32, F16, I32 = mybir.dt.float32, mybir.dt.float16, mybir.dt.int32
ACT = mybir.ActivationFunctionType
ALU = mybir.AluOpType
X = mybir.AxisListType.X

P = 128
C = 256
S = 4096
NH, D = 8, 32
CK = C // P
HALF = 4
W = 512
NW = S // W
NT = S // P
TW = W // P
E, H = 8, 682
HC = (H + P - 1) // P
HL = H - (HC - 1) * P
KR = 3 * D + 2
EPS_C, EPS_T, EPS_N = 1e-6, 1e-5, 1e-12
LO, HI = range(2)
R = S // C
RW = W // C


def group_plan():
    units = [(t, j) for t in range(NT) for j in range(HALF)]
    return [units[i:i + 3] for i in range(0, len(units), 3)]


def build(nc, x, wqkv, wproj, temp, rw, w1, w2, w3, out):
    x_v = x.rearrange("a (k p) h w -> p (a k) (h w)", p=P)
    out_v = out.rearrange("a (k p) h w -> p (a k) (h w)", p=P)
    with ExitStack() as ctx:
        def sb(name, shape, dt, c=ctx):
            return c.enter_context(nc.sbuf_tensor(name, shape, dt))

        def sem(name, c=ctx):
            return c.enter_context(nc.semaphore(name))

        ident = sb("ident", [P, P], F32)
        rwt = sb("rwt", [P, CK, E], F32)
        X1 = sb("X1", [P, NT, C], F32)
        ps = ctx.enter_context(nc.psum_tensor("ps", [P, 8, W], F32))

        with ExitStack() as ab:
            K8 = sb("K8", [P, NH, S], F16, ab)
            V = sb("V", [P, NT, C], F32, ab)
            Q8 = sb("Q8", [P, 2, HALF, W], F16, ab)
            QS = X1[:].rearrange("p t c -> p (t c)").bitcast(F16).rearrange("p (n a k w) -> p n a k w", n=NW, a=2, k=CK)
            wpt = sb("wpt", [P, CK, C], F32, ab)
            ones = sb("ones", [P, P], F32, ab)
            shh = sb("shh", [P, NH, 2], F16, ab)
            phase_a(nc, ab, sb, sem, ps, x_v, wqkv, wproj, temp, rw, ident, ones, rwt, wpt, K8, V, QS, shh, Q8, X1)
            phase_b(nc, sb, sem, ps, x_v, ident, ones, wpt, K8, V, QS, Q8, X1)
        phase_c(nc, sb, sem, ps, ident, rwt, X1, w1, w2, w3, out_v)


def phase_a(nc, ab, sb, sem, ps, x_v, wqkv, wproj, temp, rw, ident, ones, rwt, wpt, K8, V, QS, shh, Q8, X1):
    with ExitStack() as c:
        work = sb("work", [P, 16, W], F32, c)
        xin, xc, xsq, xh = work[:, 0:2], work[:, 2:4], work[:, 4:6], work[:, 6:8]
        qraw, qsq, qn = work[:, 8:12], work[:, 12:14], work[:, 14:16]
        rstd = sb("rstd", [P, W], F32, c)
        wq = sb("wq", [P, CK, 3 * C], F32, c)
        mean_w = sb("mean_w", [P, P], F32, c)
        blk = sb("blk", [P, P], F32, c)
        kl = sb("kl", [P, 2, CK, W], F16, c)
        trow = sb("trow", [P, NH], F32, c)
        tneg = sb("tneg", [P, NH], F32, c)
        scale = sb("scale", [P, 2 * CK, 1], F32, c)
        epsc = sb("epsc", [P, 1], F32, c)

        x_in, w_in = sem("x_in", c), sem("w_in", c)
        const_ready, rows_ready = sem("const_ready", c), sem("rows_ready", c)
        mean_ps, var_ps, centred, squared = sem("mean_ps", c), sem("var_ps", c), sem("centred", c), sem("squared", c)
        std_ready, rstd_ready, xh_ready = sem("std_ready", c), sem("rstd_ready", c), sem("xh_ready", c)
        qk_ps, q_copied, q_sq, n_ps, n_std, n_clamped = [sem(n, c) for n in ("qk_ps", "q_copied", "q_sq", "n_ps", "n_std", "n_clamped")]
        n_rec, q_norm, hi_ready, split_ready, v_ps, v_ready = [sem(n, c) for n in ("n_rec", "q_norm", "hi_ready", "split_ready", "v_ps", "v_ready")]
        laid, scale_ready = sem("laid", c), sem("scale_ready", c)
        MEAN, VAR, QA, QB, NA, NB, VA, VB = range(8)

        with nc.Block() as block:
            @block.sync
            def _(sp):
                sp.dma_start(wq[:], wqkv.rearrange("(k p) o -> p k o", p=P)).then_inc(w_in, 16)
                sp.dma_start(wpt[:], wproj.rearrange("(k p) o -> p k o", p=P)).then_inc(w_in, 16)
                sp.dma_start(rwt[:], rw.rearrange("(k p) o -> p k o", p=P)).then_inc(w_in, 16)
                sp.dma_start(trow[:], temp[:, :, 0].rearrange("h a -> a h").broadcast_to([P, NH])).then_inc(w_in, 16)
                sp.dma_start(xin, x_v[:, :, 0:W]).then_inc(x_in, 16)

                def lay(n, at, split):
                    sp.wait_ge(split_ready, split)
                    for r, a in enumerate((HI, HI, LO)):
                        for j in range(HALF):
                            sp.dma_start(K8[r * D:(r + 1) * D, j:NH:HALF, bass.ds(at, W)],
                                         kl[j * D:(j + 1) * D, a, :, :]).then_inc(laid, 16)

                with sp.Fori(0, NW - 1) as n:
                    at, following, read = sp.snap(n * W), sp.snap((n + 1) * W), sp.snap(CK * (n + 1))
                    split = sp.snap(4 * n + 4)
                    sp.wait_ge(centred, read)
                    sp.dma_start(xin, x_v[:, :, bass.ds(following, W)]).then_inc(x_in, 16)
                    lay(n, at, split)
                lay(NW - 1, (NW - 1) * W, 4 * NW)
                sp.wait_ge(laid, NW * 12 * 16)

            @block.gpsimd
            def _(g):
                g.memset(ident[:], 0.0).then_inc(const_ready, 1)
                g.memset(ones[:], 1.0).then_inc(const_ready, 1)
                g.memset(mean_w[:], 1.0 / C).then_inc(const_ready, 1)
                g.memset(blk[:], 0.0).then_inc(const_ready, 1)
                g.memset(epsc[:], EPS_C).then_inc(const_ready, 1)
                g.memset(scale[:, CK:2 * CK, :], 1.0).then_inc(const_ready, 1)
                g.wait_ge(const_ready, 6)
                g.affine_select(out=ident[:], in_=ident[:], compare_op=ALU.not_equal, fill=1.0, base=0,
                                pattern=[[-1, P]], channel_multiplier=1).then_inc(const_ready, 1)
                for j in range(HALF):
                    g.wait_ge(const_ready, 7 + j)
                    g.memset(blk[j * D:(j + 1) * D, j * D:(j + 1) * D], 1.0).then_inc(const_ready, 1)
                g.wait_ge(const_ready, 7 + HALF)
                g.memset(K8[3 * D:3 * D + 2, :, :], 1.0).then_inc(rows_ready, 1)

            @block.vector
            def _(v):
                v.wait_ge(w_in, 16 * 4)
                v.tensor_scalar(tneg[:], trow[:], -1.0, None, ALU.mult).then_inc(n_rec, 1)
                v.wait_ge(n_rec, 1)
                v.tensor_tensor(tneg[:], trow[:], tneg[:], ALU.min).then_inc(n_rec, 1)
                v.wait_ge(n_rec, 2)
                v.tensor_copy(shh[:, :, 0], tneg[:]).then_inc(n_rec, 1)
                v.wait_ge(n_rec, 3)
                v.tensor_tensor(shh[:, :, 1], tneg[:], shh[:, :, 0], ALU.subtract).then_inc(n_rec, 1)
                v.wait_ge(n_rec, 4)
                v.wait_ge(const_ready, 7 + HALF)
                for j in range(HALF):
                    a = slice(j * D, (j + 1) * D)
                    v.tensor_copy(scale[a, 0:CK, 0], trow[a, j:NH:HALF]).then_inc(scale_ready, 1)
                v.wait_ge(scale_ready, HALF)
                for r, rows in ((1, 2), (0, 1)):
                    a = slice(3 * D, 3 * D + rows)
                    v.tensor_copy(Q8[a].rearrange("p f j w -> p (f j) w"), shh[a, :, r:r + 1].broadcast_to([rows, NH, W])).then_inc(n_rec, 1)
                    v.wait_ge(n_rec, 6 - r)
                with v.Fori(0, NW) as n:
                    v.wait_ge(mean_ps, n + 1)
                    for k in range(CK):
                        m = v.tensor_tensor(xc[:, k], xin[:, k], ps[:, MEAN], ALU.subtract)
                        m.then_inc(centred, 1)
                    v.wait_ge(centred, CK * (n + 1))
                    v.wait_ge(std_ready, n + 1)
                    v.reciprocal(rstd[:], rstd[:]).then_inc(rstd_ready, 1)
                    v.wait_ge(rstd_ready, n + 1)
                    for k in range(CK):
                        v.tensor_tensor(xh[:, k], xc[:, k], rstd[:], ALU.mult).then_inc(xh_ready, 1)
                    for o in range(2 * CK):
                        i = o // CK
                        v.wait_ge(qk_ps, 4 * n + o + 1)
                        v.tensor_copy(qraw[:, o], ps[:, QA + o % 2]).then_inc(q_copied, 1)
                        v.wait_ge(n_std, 4 * n + o + 1)
                        v.tensor_scalar(qn[:, o % 2], qn[:, o % 2], EPS_N, None, ALU.max).then_inc(n_clamped, 1)
                        v.wait_ge(n_clamped, 4 * n + o + 1)
                        v.reciprocal(qn[:, o % 2], qn[:, o % 2]).then_inc(n_rec, 1)
                        v.wait_ge(n_rec, 4 * n + o + 7)
                        v.scalar_tensor_tensor(qraw[:, o], qraw[:, o], scale[:, o], qn[:, o % 2], ALU.mult, ALU.mult).then_inc(q_norm, 1)
                        v.wait_ge(q_norm, 4 * n + o + 1)
                        if i == 0:
                            src = qraw[:, o].rearrange("p (c n r) -> p n r c", n=NW, r=RW)
                            hi, lo = [QS[:, :, part, o % 2, :].rearrange("p n (r c) -> p n r c", r=RW)[:, :, :, bass.ds(n * (W // R), W // R)]
                                      for part in (HI, LO)]
                        else:
                            src, hi, lo = qraw[:, o], kl[:, HI, o % 2], kl[:, LO, o % 2]
                        v.tensor_copy(hi, src).then_inc(hi_ready, 1)
                        v.wait_ge(hi_ready, 4 * n + o + 1)
                        v.tensor_tensor(lo, src, hi, ALU.subtract).then_inc(split_ready, 1)
                    v.wait_ge(laid, (n + 1) * 12 * 16)

            @block.scalar
            def _(s):
                s.wait_ge(const_ready, 7 + HALF)
                with s.Fori(0, NW) as n:
                    s.wait_ge(centred, CK * (n + 1))
                    s.activation(xsq, xc, ACT.Square).then_inc(squared, 1)
                    s.wait_ge(var_ps, n + 1)
                    s.activation(rstd[:], ps[:, VAR], ACT.Sqrt, bias=epsc[:]).then_inc(std_ready, 1)
                    for o in range(2 * CK):
                        s.wait_ge(q_copied, 4 * n + o + 1)
                        s.activation(qsq[:, o % 2], qraw[:, o], ACT.Square).then_inc(q_sq, 1)
                        s.wait_ge(n_ps, 4 * n + o + 1)
                        s.activation(qn[:, o % 2], ps[:, NA + o % 2], ACT.Sqrt).then_inc(n_std, 1)
                    for t in range(TW):
                        s.wait_ge(v_ps, TW * n + t + 1)
                        s.activation(V[:, bass.ds(n * TW + t, 1), :], ps[:, VA + t % 2, 0:C].rearrange("p (a c) -> p a c", a=1), ACT.Copy).then_inc(v_ready, 1)

            @block.tensor
            def _(pe):
                pe.wait_ge(const_ready, 7 + HALF)
                pe.wait_ge(w_in, 16 * 4)
                with pe.Fori(0, NW) as n:
                    pe.wait_ge(x_in, 16 * (n + 1))
                    for k in range(CK):
                        m = pe.matmul(ps[:, MEAN], mean_w[:], xin[:, k], start=k == 0, stop=k == CK - 1)
                    m.then_inc(mean_ps, 1)
                    pe.wait_ge(squared, n + 1)
                    for k in range(CK):
                        m = pe.matmul(ps[:, VAR], mean_w[:], xsq[:, k], start=k == 0, stop=k == CK - 1)
                    m.then_inc(var_ps, 1)
                    pe.wait_ge(xh_ready, CK * (n + 1))
                    for o in range(2 * CK):
                        for k in range(CK):
                            m = pe.matmul(ps[:, QA + o % 2], wq[:, k, o * P:(o + 1) * P], xh[:, k], start=k == 0, stop=k == CK - 1)
                        m.then_inc(qk_ps, 1)
                        pe.wait_ge(q_sq, 4 * n + o + 1)
                        pe.matmul(ps[:, NA + o % 2], blk[:], qsq[:, o % 2], start=True, stop=True).then_inc(n_ps, 1)
                    for t in range(TW):
                        if t >= 2:
                            pe.wait_ge(v_ready, TW * n + t - 1)
                        for k in range(CK):
                            m = pe.matmul(ps[:, VA + t % 2, 0:C], xh[:, k, t * P:(t + 1) * P], wq[:, k, 2 * C:3 * C], start=k == 0, stop=k == CK - 1)
                        m.then_inc(v_ps, 1)
                    pe.wait_ge(v_ready, TW * (n + 1))
                    pe.wait_ge(n_std, 4 * (n + 1))


def phase_b(nc, sb, sem, ps, x_v, ident, ones, wpt, K8, V, QS, Q8, X1):
    groups = group_plan()
    NG = len(groups)
    ACC, MISC = 6, 7
    with ExitStack() as c:
        NP = 3
        Pb = sb("Pb", [P, NP, 3, W], F32, c)
        sums = sb("sums", [P, HALF, W], F32, c)
        psums = sb("psums", [P, 1, W], F32, c)
        att = sb("att", [P, W], F32, c)
        rden = sb("rden", [P, TW, HALF, 1], F32, c)
        O = sb("O", [P, TW, CK, HALF, D], F32, c)
        xres = sb("xres", [P, CK, W], F32, c)

        q_in, x_in = [sem(f"q_in{f}", c) for f in range(2)], sem("xr_in", c)
        scored, expd, pv_done = sem("scored", c), sem("expd", c), sem("pv_done", c)
        v_sum, g_sum, den_ps, den_rec, att_copied, att_ready, att_t = [sem(n, c) for n in ("v_sum", "g_sum", "den_ps", "den_rec", "att_copied", "att_ready", "att_t")]
        zeros, zeroed = sb("zeros", [P, W], F32, c), sem("zeroed", c)
        proj_ps, x1_ready = sem("proj_ps", c), sem("x1_ready", c)

        def pool_takes(t, j):
            return j == HALF - 1

        def steps(g):
            out, run = [], None
            for b, (t, j) in enumerate(groups[g]):
                if pool_takes(t, j):
                    run = None
                    continue
                if run and run[0] + run[1] == b and run[2] + run[1] == j and run[3] == (t == 0):
                    run[1] += 1
                else:
                    run = [b, 1, j, t == 0]
                    out.append(run)
            return out

        def pool_steps(g):
            return [(b, t == 0) for b, (t, j) in enumerate(groups[g]) if pool_takes(t, j)]

        VS = [len(steps(g)) for g in range(NG)]
        GS = [len(pool_steps(g)) for g in range(NG)]
        VH, GH = sum(VS), sum(GS)

        with nc.Block() as block:
            @block.sync
            def _(sp):
                def load_q(n, f):
                        for r, a in enumerate((1, 0, 1)):
                            for j in range(HALF):
                                sp.dma_start(Q8[r * D:(r + 1) * D, f, j, :],
                                             QS[j * D:(j + 1) * D, bass.ds(n, 1), a, f, :].rearrange("p b w -> p (b w)")).then_inc(q_in[f], 16)

                def load_x(at):
                    sp.dma_start(xres[:], x_v[:, :, bass.ds(at, W)]).then_inc(x_in, 16)

                load_q(0, 0)
                load_q(0, 1)
                load_x(0)
                with sp.Fori(0, NW - 1) as n:
                    chunk, at, added = sp.snap(n + 1), sp.snap((n + 1) * W), sp.snap(2 * n + 2)
                    read = [sp.snap(2 * NG * n + (f + 1) * NG) for f in range(2)]
                    for f in range(2):
                        sp.wait_ge(scored, read[f])
                        load_q(chunk, f)
                    sp.wait_ge(proj_ps, added)
                    load_x(at)
                sp.wait_ge(x_in, 16 * NW)

            def denominators(pe, n, f):
                pe.wait_ge(v_sum, (2 * n + f + 1) * VH)
                pe.wait_ge(g_sum, (2 * n + f + 1) * GH)
                for t in range(TW):
                    for j in range(HALF):
                        src = psums[:, 0] if j == HALF - 1 else sums[:, j]
                        m = pe.matmul(ps[:, MISC, HALF * t + j:HALF * t + j + 1], src[:, t * P:(t + 1) * P], ones[:, 0:1], start=True, stop=True)
                m.then_inc(den_ps, 1)

            def turn(pe, n, f):
                pe.wait_ge(den_rec, 2 * n + f + 1)
                pe.wait_ge(att_copied, 2 * n + f + 1)
                for t in range(TW):
                    m = pe.transpose(ps[:, MISC, t * P:(t + 1) * P], att[:, t * P:(t + 1) * P], ident[:])
                m.then_inc(att_t, 1)

            @block.tensor
            def _(pe):
                with pe.Fori(0, NW) as n:
                    G0 = n * (2 * NG)

                    def scores(f, g):
                        if g == 0:
                            pe.wait_ge(q_in[f], 16 * 12 * (n + 1))
                        for b, (t, j) in enumerate(groups[g]):
                            m = pe.matmul(ps[:, 3 * ((f * NG + g) % 2) + b], K8[0:KR, f * HALF + j, t * P:(t + 1) * P],
                                          Q8[0:KR, f, j, :], start=True, stop=True)
                        m.then_inc(scored, 1)

                    def values(f, g):
                        for b, (t, j) in enumerate(groups[g]):
                            m = pe.matmul(ps[j * D:(j + 1) * D, ACC], V[:, t, (f * HALF + j) * D:(f * HALF + j + 1) * D],
                                          Pb[:, (f * NG + g) % NP, b], start=t == 0, stop=t == NT - 1)
                        m.then_inc(pv_done, 1)

                    for i in range(2):
                        scores(0, i)
                    for i in range(2 * NG):
                        f, g = divmod(i, NG)
                        pe.wait_ge(expd, G0 + i + 1)
                        if i + 2 < 2 * NG:
                            scores(*divmod(i + 2, NG))
                        if g == 0:
                            if f:
                                pe.wait_ge(att_copied, 2 * n + 1)
                        values(f, g)
                        if g == 1 and f:
                            denominators(pe, n, 0)
                        if g == 5 and f:
                            turn(pe, n, 0)
                    denominators(pe, n, 1)
                    turn(pe, n, 1)
                    pe.wait_ge(att_ready, TW * (2 * n + 2))
                    pe.wait_ge(x_in, 16 * (n + 1))
                    for h in range(2):
                        if h:
                            pe.wait_ge(x1_ready, 2 * n + 1)
                        for tt in range(2):
                            t = 2 * h + tt
                            o = ps[:, MISC, tt * C:(tt + 1) * C]
                            for f in range(2):
                                pe.matmul(o, O[:, 2 * h + f, tt].rearrange("p j d -> p (j d)"), wpt[:, f, :], start=f == 0, stop=False)
                            for k in range(CK):
                                m = pe.matmul(ps[:, MISC, tt * C + k * P:tt * C + (k + 1) * P], xres[:, k, t * P:(t + 1) * P],
                                              ident[:], start=False, stop=k == CK - 1)
                        m.then_inc(proj_ps, 1)
                    pe.wait_ge(x1_ready, 2 * n + 2)

            @block.scalar
            def _(s):
                with s.Fori(0, NW) as n:
                    for i in range(2 * NG):
                        f, g = divmod(i, NG)
                        s.wait_ge(scored, n * (2 * NG) + i + 1)
                        if i >= NP:
                            u = i - NP
                            s.wait_ge(pv_done, n * (2 * NG) + u + 1)
                            s.wait_ge(v_sum, n * 2 * VH + sum(VS[h % NG] for h in range(u + 1)))
                            if sum(GS[h % NG] for h in range(u + 1)):
                                s.wait_ge(g_sum, n * 2 * GH + sum(GS[h % NG] for h in range(u + 1)))
                        nb = len(groups[g])
                        s.activation(Pb[:, i % NP, 0:nb], ps[:, 3 * (i % 2):3 * (i % 2) + nb], ACT.Exp).then_inc(expd, 1)
                    s.wait_ge(pv_done, (n + 1) * 2 * NG)
                    s.wait_ge(v_sum, (n + 1) * 2 * VH)
                    s.wait_ge(g_sum, (n + 1) * 2 * GH)
                    for h in range(2):
                        s.wait_ge(proj_ps, 2 * n + h + 1)
                        s.activation(X1[:, bass.ds(n * TW + 2 * h, 2), :], ps[:, MISC].rearrange("p (a c) -> p a c", a=2), ACT.Copy).then_inc(x1_ready, 1)

            def take(v, n, f):
                v.wait_ge(pv_done, (2 * n + f + 1) * NG)
                if f:
                    v.wait_ge(att_t, 2 * n + 1)
                v.tensor_copy(att[:], ps[:, ACC]).then_inc(att_copied, 1)

            def normalise(v, n, f):
                v.wait_ge(den_ps, 2 * n + f + 1)
                v.reciprocal(rden[:], ps[:, MISC, 0:TW * HALF].rearrange("p (t j a) -> p t j a", t=TW, j=HALF)).then_inc(den_rec, 1)
                v.wait_ge(den_rec, 2 * n + f + 1)
                v.wait_ge(att_t, 2 * n + f + 1)
                for t in range(TW):
                    m = v.tensor_tensor(O[:, t, f], ps[:, MISC, t * P:(t + 1) * P].rearrange("p (j d) -> p j d", j=HALF),
                                        rden[:, t].broadcast_to([P, HALF, D]), ALU.mult)
                    m.then_inc(att_ready, 1)

            @block.vector
            def _(v):
                with v.Fori(0, NW) as n:
                    for i in range(2 * NG):
                        f, g = divmod(i, NG)
                        v.wait_ge(expd, n * (2 * NG) + i + 1)
                        if g == 0 and f:
                            v.wait_ge(den_ps, 2 * n + 1)
                        base = n * 2 * VH + sum(VS[h % NG] for h in range(i))
                        for k, (b, m, j, first) in enumerate(steps(g)):
                            src = Pb[:, i % NP, b:b + m]
                            if first:
                                v.tensor_copy(sums[:, j:j + m], src).then_inc(v_sum, 1)
                            else:
                                v.wait_ge(v_sum, base + k)
                                v.tensor_tensor(sums[:, j:j + m], sums[:, j:j + m], src, ALU.add).then_inc(v_sum, 1)
                        if g == 6 and f:
                            normalise(v, n, 0)
                        if g == NG - 1:
                            take(v, n, f)
                    normalise(v, n, 1)

            @block.gpsimd
            def _(g_):
                g_.memset(zeros[:], 0.0).then_inc(zeroed, 1)
                g_.wait_ge(zeroed, 1)
                with g_.Fori(0, NW) as n:
                    for i in range(2 * NG):
                        f, g = divmod(i, NG)
                        if not GS[g]:
                            continue
                        g_.wait_ge(expd, n * (2 * NG) + i + 1)
                        base = n * 2 * GH + sum(GS[h % NG] for h in range(i))
                        if f and g == [GS[h] > 0 for h in range(NG)].index(True):
                            g_.wait_ge(den_ps, 2 * n + 1)
                        for k, (b, first) in enumerate(pool_steps(g)):
                            src = Pb[:, i % NP, b]
                            if first:
                                g_.tensor_tensor(psums[:, 0], src, zeros[:], ALU.add).then_inc(g_sum, 1)
                            else:
                                g_.wait_ge(g_sum, base + k)
                                g_.tensor_tensor(psums[:, 0], psums[:, 0], src, ALU.add).then_inc(g_sum, 1)


def phase_c(nc, sb, sem, ps, ident, rwt, X1, w1, w2, w3, out_v):
    w1_v = w1.rearrange("(k p) e h -> p k e h", p=P)
    w3_v = w3.rearrange("(k p) e h -> p k e h", p=P)
    with ExitStack() as c:
        gates = sb("gates", [P, NT, E], F32, c)
        mean = sb("mean", [P, NT], F32, c)
        rs = sb("rs", [P, NT], F32, c)
        W1 = sb("W1", [P, CK, E, H], F32, c)
        W3 = sb("W3", [P, CK, E, H], F32, c)
        W2 = sb("W2", [P, E, HC, C], F32, c)
        w_in, wl = sem("w_inc", c), sem("wl", c)
        xt = sb("xt", [P, CK, P], F32, c)
        xhat = sb("xhat", [P, C], F32, c)
        route(nc, sb, sem, ps, ident, rwt, X1, gates, mean, rs, xt, xhat, W1, W2, W3, w1_v, w2, w3_v, w_in)

        sg = sb("sg", [P, H], F32, c)
        hh = sb("hh", [P, H], F32, c)
        hT = sb("hT", [P, HC, P], F32, c)
        fin = sb("fin", [P, C], F32, c)
        fo = sb("fo", [P, CK, P], F32, c)
        xn, t_ps, t_cp, h1_ps, h3_ps, sg_r, h_r, ht_ps, ht_cp, y_ps, fin_r, o_ps, o_cp, o_dma, yread, ones_ = [
            sem("c_" + n, c) for n in ("xn", "t_ps", "t_cp", "h1_ps", "h3_ps", "sg_r", "h_r", "ht_ps", "ht_cp", "y_ps", "fin_r", "o_ps", "o_cp", "o_dma", "yread", "ones")]
        A1, A3, AT, AY = 0, 2, 4, 6
        halves = [(0, W), (W, H)]
        rows = [P] * (HC - 1) + [HL]
        with nc.Block() as block:
            @block.vector
            def _(v):
                v.memset(fo[:, 0, 0:1], 0.0).then_inc(o_dma, 16)
                with v.Fori(0, NT) as t:
                    v.tensor_scalar(xhat[:], X1[:, bass.ds(t, 1), :].rearrange("p a c -> p (a c)"), mean[:, bass.ds(t, 1)], rs[:, bass.ds(t, 1)], ALU.subtract, ALU.mult).then_inc(xn, 1)
                    v.wait_ge(t_ps, t + 1)
                    v.tensor_copy(xt[:], ps[:, 7, 0:C].rearrange("p (k m) -> p k m", k=CK)).then_inc(t_cp, 1)
                    for e in range(E):
                        v.wait_ge(sg_r, E * t + e + 1)
                        v.wait_ge(h3_ps, E * t + e + 1)
                        for i, (a, b) in enumerate(halves):
                            m = v.scalar_tensor_tensor(hh[:, a:b], ps[:, A3 + i, 0:b - a], gates[:, bass.ds(t, 1), e], sg[:, a:b], ALU.mult, ALU.mult)
                            m.then_inc(h_r, 1)
                        v.wait_ge(ht_ps, E * t + e + 1)
                        v.tensor_copy(hT[:, 0:4], ps[:, AT].rearrange("p (k m) -> p k m", k=4)).then_inc(ht_cp, 1)
                        v.tensor_copy(hT[:, 4], ps[:, AT + 1, 0:P]).then_inc(ht_cp, 1)
                        v.tensor_copy(hT[0:HL, 5], ps[0:HL, AT + 1, P:2 * P]).then_inc(ht_cp, 1)
                    v.wait_ge(y_ps, t + 1)
                    v.tensor_tensor(fin[:], X1[:, bass.ds(t, 1), :].rearrange("p a c -> p (a c)"), ps[:, AY, 0:C], ALU.add).then_inc(fin_r, 1)
                    v.wait_ge(o_ps, t + 1)
                    v.wait_ge(o_dma, 16 * (t + 1))
                    v.tensor_copy(fo[:], ps[:, 7, C:2 * C].rearrange("p (k m) -> p k m", k=CK)).then_inc(o_cp, 1)

            @block.scalar
            def _(s):
                with s.Fori(0, NT) as t:
                    for e in range(E):
                        s.wait_ge(h1_ps, E * t + e + 1)
                        for i, (a, b) in enumerate(halves):
                            m = s.activation(sg[:, a:b], ps[:, A1 + i, 0:b - a], ACT.Silu)
                        m.then_inc(sg_r, 1)
                        s.wait_ge(h_r, 2 * (E * t + e + 1))

            @block.sync
            def _(sp):
                with sp.Fori(0, NT) as t:
                    at, ready = sp.snap(t * P), sp.snap(t + 1)
                    sp.wait_ge(o_cp, ready)
                    sp.dma_start(out_v[:, :, bass.ds(at, P)], fo[:]).then_inc(o_dma, 16)
                sp.wait_ge(o_dma, 16 * (NT + 1))

            @block.tensor
            def _(pe):
                with pe.Fori(0, NT) as t:
                    pe.wait_ge(xn, t + 1)
                    for k in range(CK):
                        m = pe.transpose(ps[:, 7, k * P:(k + 1) * P], xhat[:, k * P:(k + 1) * P], ident[:])
                    m.then_inc(t_ps, 1)
                    pe.wait_ge(t_cp, t + 1)
                    for e in range(E):
                        for bank, wt, s_ in ((A1, W1, h1_ps), (A3, W3, h3_ps)):
                            for i, (a, b) in enumerate(halves):
                                for k in range(CK):
                                    m = pe.matmul(ps[:, bank + i, 0:b - a], xt[:, k], wt[:, k, e, a:b], start=k == 0, stop=k == CK - 1)
                            m.then_inc(s_, 1)
                        pe.wait_ge(h_r, 2 * (E * t + e + 1))
                        for k in range(HC):
                            m = pe.transpose(ps[0:rows[k], AT + k // 4, (k % 4) * P:(k % 4 + 1) * P], hh[:, k * P:k * P + rows[k]], ident[:])
                        m.then_inc(ht_ps, 1)
                        pe.wait_ge(ht_cp, 3 * (E * t + e + 1))
                        for k in range(HC):
                            m = pe.matmul(ps[:, AY, 0:C], hT[0:rows[k], k], W2[0:rows[k], e, k, :], start=e == 0 and k == 0, stop=e == E - 1 and k == HC - 1)
                    m.then_inc(y_ps, 1)
                    pe.wait_ge(fin_r, t + 1)
                    for k in range(CK):
                        m = pe.transpose(ps[:, 7, C + k * P:C + (k + 1) * P], fin[:, k * P:(k + 1) * P], ident[:])
                    m.then_inc(o_ps, 1)
                    pe.wait_ge(o_cp, t + 1)


def route(nc, sb, sem, ps, ident, rwt, X1, gates, mean, rs, xt, xhat, W1, W2, W3, w1_v, w2, w3_v, w_in):
    with ExitStack() as c:
        st = sb("st", [P, NT, 6], F32, c)
        mv = sb("mv", [P, NT, 2], F32, c)
        lg = sb("lg", [P, NT, E], F32, c)
        pr = sb("pr", [P, NT, E], F32, c)
        m1 = sb("m1", [P, NT], F32, c)
        m2 = sb("m2", [P, NT], F32, c)
        mean2 = sb("mean2", [P, NT], F32, c)
        rev = sb("rev", [P, NT, E], F32, c)
        revi = sb("revi", [P, NT, E], I32, c)
        tmp = sb("tmp", [P, NT, E], F32, c)
        oh1 = sb("oh1", [P, NT, E], F32, c)
        oh2 = sb("oh2", [P, NT, E], F32, c)
        epst = sb("epst", [P, 1], F32, c)
        stat, var_r, std_r, xn, t_ps, t_cp, l_ps, l_cp, it, ex, mx, ch, eps_r = [sem("r_" + n, c) for n in (
            "stat", "var", "std", "xn", "t_ps", "t_cp", "l_ps", "l_cp", "it", "ex", "mx", "ch", "eps")]
        aggr = sem("r_aggr", c)
        B3 = [P, NT, E]
        with nc.Block() as block:
            @block.sync
            def _(sp):
                for e in range(E):
                    for k in range(CK):
                        sp.dma_start(W1[:, k, e, :], w1_v[:, k, e, :]).then_inc(w_in, 16)
                        sp.dma_start(W3[:, k, e, :], w3_v[:, k, e, :]).then_inc(w_in, 16)
                    sp.dma_start(W2[:, e, 0:HC - 1, :], w2[e, 0:(HC - 1) * P, :].rearrange("(k p) c -> p k c", p=P)).then_inc(w_in, 16)
                    sp.dma_start(W2[0:HL, e, HC - 1, :], w2[e, (HC - 1) * P:H, :]).then_inc(w_in, 16)
                sp.wait_ge(w_in, 16 * 6 * E)

            @block.gpsimd
            def _(g):
                g.iota(revi[:], pattern=[[0, NT], [-1, E]], base=E, channel_multiplier=0).then_inc(it, 1)
                g.memset(epst[:], EPS_T).then_inc(eps_r, 1)

            @block.vector
            def _(v):
                n_ch = [0]

                def chain(ins):
                    n_ch[0] += 1
                    ins.then_inc(ch, 1)
                    v.wait_ge(ch, n_ch[0])

                for t in range(NT):
                    v.bn_stats(st[:, t], X1[:, t, :]).then_inc(stat, 1)
                for t in range(NT):
                    v.wait_ge(stat, t + 1)
                    v.bn_aggr(mv[:, t, :], st[:, t]).then_inc(aggr, 1)
                v.wait_ge(aggr, NT)
                v.tensor_copy(mean[:], mv[:, :, 0]).then_inc(var_r, 1)
                v.wait_ge(std_r, 1)
                chain(v.reciprocal(rs[:], rs[:]))
                with v.Fori(0, NT) as t:
                    v.tensor_scalar(xhat[:], X1[:, bass.ds(t, 1), :].rearrange("p a c -> p (a c)"), mean[:, bass.ds(t, 1)], rs[:, bass.ds(t, 1)], ALU.subtract, ALU.mult).then_inc(xn, 1)
                    v.wait_ge(t_ps, t + 1)
                    v.tensor_copy(xt[:], ps[:, 7, 0:C].rearrange("p (k m) -> p k m", k=CK)).then_inc(t_cp, 1)
                    v.wait_ge(l_ps, t + 1)
                    v.tensor_copy(lg[:, bass.ds(t, 1), :], ps[:, 6:7, 0:E]).then_inc(l_cp, 1)
                v.wait_ge(l_cp, NT)
                chain(v.tensor_reduce(m1[:], lg[:], X, ALU.max))
                chain(v.tensor_tensor(lg[:], lg[:], m1[:].rearrange("p (a b) -> p a b", b=1).broadcast_to(B3), ALU.subtract))
                v.memset(tmp[:, 0, 0:1], 0.0).then_inc(mx, 1)
                v.wait_ge(mx, 1)
                v.wait_ge(ex, 1)
                chain(v.tensor_reduce(m1[:], pr[:], X, ALU.add))
                chain(v.reciprocal(m1[:], m1[:]))
                chain(v.tensor_tensor(pr[:], pr[:], m1[:].rearrange("p (a b) -> p a b", b=1).broadcast_to(B3), ALU.mult))
                v.wait_ge(it, 1)
                chain(v.tensor_copy(rev[:], revi[:]))

                def pick(best, oh, probs):
                    chain(v.tensor_reduce(best[:], probs[:], X, ALU.max))
                    b = best[:].rearrange("p (a b) -> p a b", b=1).broadcast_to(B3)
                    chain(v.tensor_tensor(oh[:], probs[:], b, ALU.is_equal))
                    chain(v.tensor_tensor(oh[:], oh[:], rev[:], ALU.mult))
                    chain(v.tensor_reduce(mean2[:], oh[:], X, ALU.max))
                    chain(v.tensor_tensor(oh[:], rev[:], mean2[:].rearrange("p (a b) -> p a b", b=1).broadcast_to(B3), ALU.is_equal))

                pick(m1, oh1, pr)
                chain(v.tensor_scalar(tmp[:], oh1[:], -1.0, 1.0, ALU.mult, ALU.add))
                chain(v.tensor_tensor(tmp[:], tmp[:], pr[:], ALU.mult))
                chain(v.tensor_tensor(tmp[:], tmp[:], oh1[:], ALU.subtract))
                pick(m2, oh2, tmp)
                chain(v.tensor_tensor(mean2[:], m1[:], m2[:], ALU.add))
                chain(v.tensor_scalar(mean2[:], mean2[:], 1e-9, None, ALU.add))
                chain(v.reciprocal(mean2[:], mean2[:]))
                chain(v.tensor_tensor(oh1[:], oh1[:], oh2[:], ALU.add))
                chain(v.tensor_tensor(gates[:], oh1[:], pr[:], ALU.mult))
                chain(v.tensor_tensor(gates[:], gates[:], mean2[:].rearrange("p (a b) -> p a b", b=1).broadcast_to(B3), ALU.mult))

            @block.scalar
            def _(s):
                s.wait_ge(eps_r, 1)
                s.wait_ge(var_r, 1)
                s.activation(rs[:], mv[:, :, 1], ACT.Sqrt, bias=epst[:]).then_inc(std_r, 1)
                s.wait_ge(mx, 1)
                s.activation(pr[:], lg[:], ACT.Exp).then_inc(ex, 1)

            @block.tensor
            def _(pe):
                with pe.Fori(0, NT) as t:
                    pe.wait_ge(xn, t + 1)
                    for k in range(CK):
                        m = pe.transpose(ps[:, 7, k * P:(k + 1) * P], xhat[:, k * P:(k + 1) * P], ident[:])
                    m.then_inc(t_ps, 1)
                    pe.wait_ge(t_cp, t + 1)
                    for k in range(CK):
                        m = pe.matmul(ps[:, 6, 0:E], xt[:, k], rwt[:, k], start=k == 0, stop=k == CK - 1)
                    m.then_inc(l_ps, 1)
                    pe.wait_ge(l_cp, t + 1)


def kernel(**inputs):
    import numpy as np
    import concourse.bacc as bacc
    from concourse.bass_utils import run_bass_kernel_spmd

    laid = {
        "x": inputs["x"],
        "wqkv": np.transpose(inputs["L0_conv_w_qkv"]),
        "wproj": np.transpose(inputs["L0_conv_w_proj"]),
        "temp": inputs["L0_conv_temperature"],
        "rw": np.transpose(inputs["L0_ffn_router_w"]),
        "w1": np.transpose(inputs["L0_ffn_w1"], (2, 0, 1)),
        "w2": np.transpose(inputs["L0_ffn_w2"], (0, 2, 1)),
        "w3": np.transpose(inputs["L0_ffn_w3"], (2, 0, 1)),
    }
    nc = bacc.Bacc("TRN2", target_bir_lowering=False, num_devices=1)
    arrays, args = {}, []
    for name, a in laid.items():
        a = np.ascontiguousarray(a)
        arrays[f"in_{name}"] = a
        args.append(nc.dram_tensor(f"in_{name}", a.shape, mybir.dt.from_np(a.dtype), kind="ExternalInput").ap())
    args.append(nc.dram_tensor("result", (1, C, 64, 64), F32, kind="ExternalOutput").ap())
    build(nc, *args)
    r = run_bass_kernel_spmd(nc, [arrays], core_ids=[0])
    return r.results[0]["result"]
```

```python
from contextlib import ExitStack

import concourse.bass as bass
from concourse import mybir

F32, F16, I32 = mybir.dt.float32, mybir.dt.float16, mybir.dt.int32
ACT = mybir.ActivationFunctionType
ALU = mybir.AluOpType
X = mybir.AxisListType.X

P = 128
C = 256
S = 4096
NH, D = 8, 32
CK = C // P
HALF = 4
W = 512
NW = S // W
NT = S // P
TW = W // P
E, H = 8, 682
HC = (H + P - 1) // P
HL = H - (HC - 1) * P
KR = 3 * D + 2
NTS = (2 * S + E * (P - 1)) // P
NS = (NTS + 1) * P
EPS_C, EPS_T, EPS_N = 1e-6, 1e-5, 1e-12
LO, HI = range(2)
R = S // C
RW = W // C


def group_plan():
    units = [(t, j) for t in range(NT) for j in range(HALF)]
    return [units[i:i + 3] for i in range(0, len(units), 3)]


def build(nc, x, wqkv, wproj, temp, rw, w1, w2, w3, out):
    x_v = x.rearrange("a (k p) h w -> p (a k) (h w)", p=P)
    out_v = out.rearrange("a (k p) h w -> p (a k) (h w)", p=P)
    sorted_x = nc.dram_tensor("sorted_x", (NS, C), F32, kind="Internal").ap()
    sorted_y = nc.dram_tensor("sorted_y", (NTS * P, C), F32, kind="Internal").ap()
    with ExitStack() as ctx:
        def sb(name, shape, dt, c=ctx):
            return c.enter_context(nc.sbuf_tensor(name, shape, dt))

        def sem(name, c=ctx):
            return c.enter_context(nc.semaphore(name))

        ident = sb("ident", [P, P], F32)
        rwt = sb("rwt", [P, CK, E], F32)
        X1 = sb("X1", [P, NT, C], F32)
        ps = ctx.enter_context(nc.psum_tensor("ps", [P, 8, W], F32))

        with ExitStack() as ab:
            K8 = sb("K8", [P, NH, S], F16, ab)
            V = sb("V", [P, NT, C], F32, ab)
            Q8 = sb("Q8", [P, 2, HALF, W], F16, ab)
            QS = X1[:].rearrange("p t c -> p (t c)").bitcast(F16).rearrange("p (n a k w) -> p n a k w", n=NW, a=2, k=CK)
            wpt = sb("wpt", [P, CK, C], F32, ab)
            ones = sb("ones", [P, P], F32, ab)
            sel = sb("sel", [P, HALF], F32, ab)
            shh = sb("shh", [P, NH, 2], F16, ab)
            phase_a(nc, ab, sb, sem, ps, x_v, wqkv, wproj, temp, rw, ident, ones, sel, rwt, wpt, K8, V, QS, shh, Q8, X1)
            phase_b(nc, sb, sem, ps, x_v, ident, ones, sel, wpt, K8, V, QS, Q8, X1, sorted_x)
        phase_c(nc, sb, sem, ps, ident, rwt, X1, w1, w2, w3, sorted_x, sorted_y, out_v)


def phase_a(nc, ab, sb, sem, ps, x_v, wqkv, wproj, temp, rw, ident, ones, sel, rwt, wpt, K8, V, QS, shh, Q8, X1):
    with ExitStack() as c:
        xin = sb("xin", [P, CK, W], F32, c)
        xc = sb("xc", [P, 2, CK, W], F32, c)
        xsq = sb("xsq", [P, CK, W], F32, c)
        qraw = sb("qraw", [P, 2 * CK, W], F32, c)
        qsq = sb("qsq", [P, 2 * CK, W], F32, c)
        nrm = sb("nrm", [P, W], F32, c)
        std = sb("std", [P, W], F32, c)
        rn = sb("rn", [P, W], F32, c)
        stdt = sb("stdt", [P, TW], F32, c)
        rt = sb("rt", [P, 2, TW], F32, c)
        wq = sb("wq", [P, CK, 3 * C], F32, c)
        mean_w = sb("mean_w", [P, P], F32, c)
        grp = sb("grp", [P, D], F32, c)
        back = sb("back", [P, HALF, D], F32, c)
        kl = sb("kl", [P, 2, CK, W], F16, c)
        trow = sb("trow", [P, NH], F32, c)
        tneg = sb("tneg", [P, NH], F32, c)
        scale = sb("scale", [P, 2 * CK, 1], F32, c)
        epsc = sb("epsc", [P, 1], F32, c)

        x_in, w_in, const_ready, shift_ready, scale_ready = [sem(n, c) for n in ("x_in", "w_in", "const_ready", "shift_ready", "scale_ready")]
        mean_ps, centred, squared, var_ps, std_ready, stdt_ready, rt_ready = [sem(n, c) for n in (
            "mean_ps", "centred", "squared", "var_ps", "std_ready", "stdt_ready", "rt_ready")]
        qk_ps, q_copied, q_sq, n_ps, n_sqrt, clamped, rn_ready, back_ps = [sem(n, c) for n in (
            "qk_ps", "q_copied", "q_sq", "n_ps", "n_sqrt", "clamped", "rn_ready", "back_ps")]
        q_norm, hi_ready, split_ready, v_ps, v_ready, laid = [sem(n, c) for n in ("q_norm", "hi_ready", "split_ready", "v_ps", "v_ready", "laid")]
        LN, NRM, QK, BACK = 0, 1, 2, 4
        OC = 2 * CK
        CONSTS = 7 + 2 + HALF + HALF

        def rounds(eng, chunk):
            chunk(0, 0, first=True)
            with eng.Fori(1, NW - 1, 2) as n:
                chunk(n, 1)
                chunk(n + 1, 0)
            chunk(NW - 1, 1, last=True)

        with nc.Block() as block:
            @block.sync
            def _(sp):
                def load_x(at):
                    sp.dma_start(xin[:], x_v[:, :, bass.ds(at, W)]).then_inc(x_in, 16)

                def lay(at):
                    for r, a in enumerate((HI, HI, LO)):
                        for j in range(HALF):
                            sp.dma_start(K8[r * D:(r + 1) * D, j:NH:HALF, bass.ds(at, W)],
                                         kl[j * D:(j + 1) * D, a, :, :]).then_inc(laid, 16)

                load_x(0)
                sp.dma_start(trow[:], temp[:, :, 0].rearrange("h a -> a h").broadcast_to([P, NH])).then_inc(w_in, 16)
                sp.dma_start(wq[:], wqkv.rearrange("(k p) o -> p k o", p=P)).then_inc(w_in, 16)
                sp.dma_start(wpt[:], wproj.rearrange("(k p) o -> p k o", p=P)).then_inc(w_in, 16)
                sp.dma_start(rwt[:], rw.rearrange("(k p) o -> p k o", p=P)).then_inc(w_in, 16)
                sp.wait_ge(centred, CK)
                load_x(W)
                sp.wait_ge(centred, 2 * CK)
                load_x(2 * W)
                with sp.Fori(1, NW - 2) as n:
                    before, after, split, read = sp.snap((n - 1) * W), sp.snap((n + 2) * W), sp.snap(OC * n), sp.snap(CK * (n + 2))
                    sp.wait_ge(split_ready, split)
                    lay(before)
                    sp.wait_ge(centred, read)
                    load_x(after)
                for m in range(NW - 3, NW):
                    sp.wait_ge(split_ready, OC * (m + 1))
                    lay(m * W)
                sp.wait_ge(laid, NW * 12 * 16)

            @block.gpsimd
            def _(g):
                g.memset(ident[:], 0.0).then_inc(const_ready, 1)
                g.memset(ones[:], 1.0).then_inc(const_ready, 1)
                g.memset(mean_w[:], 1.0 / C).then_inc(const_ready, 1)
                g.memset(grp[:], 0.0).then_inc(const_ready, 1)
                g.memset(back[:], 0.0).then_inc(const_ready, 1)
                g.memset(epsc[:], EPS_C).then_inc(const_ready, 1)
                g.memset(sel[:], 0.0).then_inc(const_ready, 1)
                g.wait_ge(const_ready, 7)
                g.affine_select(out=ident[:], in_=ident[:], compare_op=ALU.not_equal, fill=1.0, base=0,
                                pattern=[[-1, P]], channel_multiplier=1).then_inc(const_ready, 1)
                g.affine_select(out=sel[:], in_=sel[:], compare_op=ALU.not_equal, fill=1.0, base=0,
                                pattern=[[-D, HALF]], channel_multiplier=1).then_inc(const_ready, 1)
                for j in range(HALF):
                    a = slice(j * D, (j + 1) * D)
                    g.wait_ge(const_ready, 9 + 2 * j)
                    g.memset(grp[a, j * D // HALF:(j + 1) * D // HALF], 1.0).then_inc(const_ready, 1)
                    g.wait_ge(const_ready, 10 + 2 * j)
                    g.affine_select(out=back[a], in_=back[a], compare_op=ALU.not_equal, fill=1.0, base=0,
                                    pattern=[[-D // HALF, HALF], [0, D]], channel_multiplier=1).then_inc(const_ready, 1)
                g.wait_ge(const_ready, CONSTS)
                g.memset(K8[3 * D:3 * D + 2, :, :], 1.0).then_inc(const_ready, 1)
                g.wait_ge(const_ready, CONSTS + 1)

            @block.vector
            def _(v):
                def centre(n, b):
                    v.wait_ge(mean_ps, n + 1)
                    for k in range(CK):
                        v.tensor_tensor(xc[:, b, k], xin[:, k], ps[:, LN], ALU.subtract).then_inc(centred, 1)

                def inverse_std(n, b):
                    v.wait_ge(stdt_ready, n + 1)
                    v.reciprocal(rt[:, b], stdt[:]).then_inc(rt_ready, 1)

                def finish(n):
                    v.wait_ge(back_ps, n + 1)
                    for o in range(OC):
                        v.scalar_tensor_tensor(qraw[:, o], qraw[:, o], scale[:, o], ps[:, BACK + o], ALU.mult, ALU.mult).then_inc(q_norm, 1)
                    for o in range(OC):
                        if o < CK:
                            src = qraw[:, o].rearrange("p (c n r) -> p n r c", n=NW, r=RW)
                            hi, lo = [QS[:, :, part, o, :].rearrange("p n (r c) -> p n r c", r=RW)[:, :, :, bass.ds(n * (W // R), W // R)]
                                      for part in (HI, LO)]
                        else:
                            if o == CK and not (isinstance(n, int) and n == 0):
                                v.wait_ge(laid, n * 12 * 16)
                            src, hi, lo = qraw[:, o], kl[:, HI, o - CK], kl[:, LO, o - CK]
                        v.wait_ge(q_norm, OC * n + o + 1)
                        v.tensor_copy(hi, src).then_inc(hi_ready, 1)
                        v.wait_ge(hi_ready, OC * n + o + 1)
                        v.tensor_tensor(lo, src, hi, ALU.subtract).then_inc(split_ready, 1)

                def inverse_norms(n):
                    v.wait_ge(n_sqrt, n + 1)
                    v.wait_ge(std_ready, n + 1)
                    v.scalar_tensor_tensor(nrm[:], std[:], EPS_N, nrm[:], ALU.mult, ALU.max).then_inc(clamped, 1)
                    v.wait_ge(clamped, n + 1)
                    v.reciprocal(rn[:], nrm[:]).then_inc(rn_ready, 1)

                def chunk(n, b, first=False, last=False):
                    if not first:
                        finish(n - 1)
                    if not last:
                        centre(n + 1, 1 - b)
                    inverse_norms(n)
                    if not last:
                        inverse_std(n + 1, 1 - b)

                v.wait_ge(const_ready, CONSTS)
                v.wait_ge(w_in, 16 * 4)
                centre(0, 0)
                v.memset(scale[:, CK:OC, :], 1.0).then_inc(scale_ready, 1)
                for j in range(HALF):
                    a = slice(j * D, (j + 1) * D)
                    v.tensor_copy(scale[a, 0:CK, 0], trow[a, j:NH:HALF]).then_inc(scale_ready, 1)
                v.tensor_scalar(tneg[:], trow[:], -1.0, None, ALU.mult).then_inc(shift_ready, 1)
                v.wait_ge(shift_ready, 1)
                v.tensor_tensor(tneg[:], trow[:], tneg[:], ALU.min).then_inc(shift_ready, 1)
                v.wait_ge(shift_ready, 2)
                v.tensor_copy(shh[:, :, 0], tneg[:]).then_inc(shift_ready, 1)
                v.wait_ge(shift_ready, 3)
                v.tensor_tensor(shh[:, :, 1], tneg[:], shh[:, :, 0], ALU.subtract).then_inc(shift_ready, 1)
                v.wait_ge(shift_ready, 4)
                for r, rows in ((1, 2), (0, 1)):
                    a = slice(3 * D, 3 * D + rows)
                    v.tensor_copy(Q8[a].rearrange("p f j w -> p (f j) w"), shh[a, :, r:r + 1].broadcast_to([rows, NH, W])).then_inc(shift_ready, 1)
                    v.wait_ge(shift_ready, 6 - r)
                v.wait_ge(scale_ready, 1 + HALF)
                inverse_std(0, 0)
                rounds(v, chunk)
                finish(NW - 1)

            @block.scalar
            def _(s):
                def square_x(n, b):
                    s.wait_ge(centred, CK * (n + 1))
                    s.activation(xsq[:], xc[:, b], ACT.Square).then_inc(squared, 1)

                def stds(n):
                    s.wait_ge(var_ps, n + 1)
                    if not (isinstance(n, int) and n == 0):
                        s.wait_ge(clamped, n)
                        s.wait_ge(rt_ready, n)
                    s.activation(std[:], ps[:, LN], ACT.Sqrt, bias=epsc[:]).then_inc(std_ready, 1)
                    s.activation(stdt[:], ps[:, NRM, 0:TW], ACT.Sqrt, bias=epsc[:]).then_inc(stdt_ready, 1)

                def chunk(n, b, first=False, last=False):
                    for o in range(OC):
                        s.wait_ge(qk_ps, OC * n + o + 1)
                        if not first:
                            s.wait_ge(split_ready, OC * (n - 1) + o + 1)
                        s.activation(qraw[:, o], ps[:, QK + o % 2], ACT.Copy).then_inc(q_copied, 1)
                        s.wait_ge(q_copied, OC * n + o + 1)
                        s.activation(qsq[:, o], qraw[:, o], ACT.Square).then_inc(q_sq, 1)
                    if not last:
                        square_x(n + 1, 1 - b)
                    s.wait_ge(n_ps, n + 1)
                    if not first:
                        s.wait_ge(rn_ready, n)
                    s.activation(nrm[:], ps[:, NRM], ACT.Sqrt).then_inc(n_sqrt, 1)
                    s.wait_ge(rt_ready, n + 1)
                    for t in range(TW):
                        if t % 2 == 0:
                            s.wait_ge(v_ps, 2 * n + t // 2 + 1)
                        s.activation(V[:, bass.ds(n * TW + t, 1), :], ps[:, QK + t // 2, (t % 2) * C:(t % 2 + 1) * C].rearrange("p (a c) -> p a c", a=1),
                                     ACT.Copy, scale=rt[:, b, t:t + 1]).then_inc(v_ready, 1)
                    if not last:
                        stds(n + 1)

                s.wait_ge(const_ready, CONSTS)
                square_x(0, 0)
                stds(0)
                rounds(s, chunk)

            @block.tensor
            def _(pe):
                def mean(n):
                    pe.wait_ge(x_in, 16 * (n + 1))
                    if not (isinstance(n, int) and n == 0):
                        pe.wait_ge(std_ready, n)
                    for k in range(CK):
                        m = pe.matmul(ps[:, LN], mean_w[:], xin[:, k], start=k == 0, stop=k == CK - 1)
                    m.then_inc(mean_ps, 1)

                def variance(n):
                    pe.wait_ge(squared, n + 1)
                    if not (isinstance(n, int) and n == 0):
                        pe.wait_ge(n_sqrt, n)
                    for k in range(CK):
                        pe.matmul(ps[:, LN], mean_w[:], xsq[:, k], start=k == 0, stop=k == CK - 1)
                    for t in range(TW):
                        for k in range(CK):
                            m = pe.matmul(ps[:, NRM, t:t + 1], xsq[:, k, t * P:(t + 1) * P], mean_w[:, 0:1], start=k == 0, stop=k == CK - 1)
                    m.then_inc(var_ps, 1)

                def spread(n):
                    pe.wait_ge(rn_ready, n + 1)
                    for o in range(OC):
                        a = slice(o * D, (o + 1) * D)
                        m = pe.matmul(ps[:, BACK + o], back[a].rearrange("p j d -> p (j d)"), rn[a], start=True, stop=True)
                    m.then_inc(back_ps, 1)

                def chunk(n, b, first=False, last=False):
                    if not first:
                        spread(n - 1)
                    pe.wait_ge(centred, CK * (n + 1))
                    for o in range(OC):
                        if o >= 2:
                            pe.wait_ge(q_copied, OC * n + o - 1)
                        elif not first:
                            pe.wait_ge(v_ready, TW * n - 2 + 2 * o)
                        for k in range(CK):
                            m = pe.matmul(ps[:, QK + o % 2], wq[:, k, o * P:(o + 1) * P], xc[:, b, k], start=k == 0, stop=k == CK - 1)
                        m.then_inc(qk_ps, 1)
                    if not last:
                        mean(n + 1)
                    pe.wait_ge(q_sq, OC * (n + 1))
                    pe.wait_ge(stdt_ready, n + 1)
                    for o in range(OC):
                        m = pe.matmul(ps[o * D:(o + 1) * D, NRM], grp[:], qsq[:, o], start=True, stop=True)
                    m.then_inc(n_ps, 1)
                    for t in range(TW):
                        for k in range(CK):
                            m = pe.matmul(ps[:, QK + t // 2, (t % 2) * C:(t % 2 + 1) * C], xc[:, b, k, t * P:(t + 1) * P], wq[:, k, 2 * C:3 * C],
                                          start=k == 0, stop=k == CK - 1)
                        if t % 2:
                            m.then_inc(v_ps, 1)
                    if not last:
                        variance(n + 1)

                pe.wait_ge(const_ready, CONSTS)
                pe.wait_ge(w_in, 16 * 4)
                mean(0)
                variance(0)
                rounds(pe, chunk)
                spread(NW - 1)


def phase_b(nc, sb, sem, ps, x_v, ident, ones, sel, wpt, K8, V, QS, Q8, X1, sorted_x):
    groups = group_plan()
    NG = len(groups)
    N2 = 2 * NG
    AT_DEN, AT_TURN, AT_PROJ, AT_X1, AT_SUMS = 5, 7, (9, 12), (11, 14), 39
    PE_TILES = (12, 16, 20, 24, 27)
    NP = 5
    short = -N2 % NP
    slots = [k for b in range((N2 + short) // NP) for k in range(NP - (b >= (N2 + short) // NP - short))]
    assert len(slots) == N2

    def last_user(i):
        u = i - 1
        while slots[u % N2] != slots[i]:
            u -= 1
        return u

    def adds(g):
        out = []
        for b, (t, j) in enumerate(groups[g]):
            if t in PE_TILES:
                continue
            if out and out[-1][0] + out[-1][1] == b and out[-1][2] + out[-1][1] == j:
                out[-1][1] += 1
            else:
                out.append([b, 1, j, t == 0])
        return out

    VS = [len(adds(i % NG)) for i in range(N2)]
    VH = sum(VS[:NG])

    with ExitStack() as c:
        Pb = sb("Pb", [P, NP, 3, W], F32, c)
        sums = sb("sums", [P, 2, HALF, W], F32, c)
        pesums = sb("pesums", [P, W], F32, c)
        att = sb("att", [P, W], F32, c)
        rden = sb("rden", [P, TW, HALF, 1], F32, c)
        O = sb("O", [P, TW, CK, HALF, D], F32, c)
        xres = sb("xres", [P, CK, W], F32, c)
        zeros = sb("zeros", [P, C], F32, c)

        q_in = [sem(f"q_in{f}", c) for f in range(2)]
        x_in, scored, expd, pv_done, v_sum, pesum_copied, den_ps, den_rec, att_copied, att_t, att_ready, proj_ps, x1_ready, zeroed, cleared = [
            sem(n, c) for n in ("xr_in", "scored", "expd", "pv_done", "v_sum", "pesum_copied", "den_ps", "den_rec", "att_copied", "att_t",
                                "att_ready", "proj_ps", "x1_ready", "zeroed", "cleared")]

        def bank(f):
            return 6 + f

        with nc.Block() as block:
            @block.sync
            def _(sp):
                def load_q(n, f):
                    for r, a in enumerate((HI, LO, HI)):
                        for j in range(HALF):
                            sp.dma_start(Q8[r * D:(r + 1) * D, f, j, :],
                                         QS[j * D:(j + 1) * D, bass.ds(n, 1), a, f, :].rearrange("p b w -> p (b w)")).then_inc(q_in[f], 16)

                def load_x(at):
                    sp.dma_start(xres[:], x_v[:, :, bass.ds(at, W)]).then_inc(x_in, 16)

                load_q(0, 0)
                load_q(0, 1)
                load_x(0)
                sp.wait_ge(zeroed, 1)
                for i in range(NTS + 1):
                    sp.dma_start(sorted_x[i * P:(i + 1) * P, :], zeros[:]).then_inc(cleared, 16)
                with sp.Fori(0, NW - 1) as n:
                    chunk, at, added = sp.snap(n + 1), sp.snap((n + 1) * W), sp.snap(2 * n + 2)
                    read = [sp.snap(N2 * n + (f + 1) * NG) for f in range(2)]
                    for f in range(2):
                        sp.wait_ge(scored, read[f])
                        load_q(chunk, f)
                    sp.wait_ge(proj_ps, added)
                    load_x(at)
                sp.wait_ge(scored, N2 * (NW - 1) + NG)
                load_q(NW - 1, 0)
                sp.wait_ge(x_in, 16 * NW)
                sp.wait_ge(cleared, 16 * (NTS + 1))

            @block.tensor
            def _(pe):
                def scores(n, i, base=0):
                    f, g = divmod(i, NG)
                    if g == 0:
                        pe.wait_ge(q_in[f], 16 * 3 * HALF * (n + base + 1))
                    for b, (t, j) in enumerate(groups[g]):
                        m = pe.matmul(ps[:, 3 * (i % 2) + b], K8[0:KR, f * HALF + j, t * P:(t + 1) * P], Q8[0:KR, f, j, :], start=True, stop=True)
                    m.then_inc(scored, 1)

                def values(n, i, first):
                    f, g = divmod(i, NG)
                    if g == 0 and not (first and f == 0):
                        pe.wait_ge(pesum_copied, 2 * n + f)
                    for b, (t, j) in enumerate(groups[g]):
                        rows, e = slice(j * D, (j + 1) * D), Pb[:, slots[i], b]
                        if (t, j) == (PE_TILES[0], 0) and f:
                            pe.wait_ge(att_ready, TW * (2 * n + 1))
                        if (t, j) == (PE_TILES[0], 0) and not f and not first:
                            pe.wait_ge(x1_ready, 2 * n)
                        m = pe.matmul(ps[rows, bank(f)], V[:, t, (f * HALF + j) * D:(f * HALF + j + 1) * D], e, start=t == 0, stop=t == NT - 1)
                        if t in PE_TILES:
                            m = pe.matmul(ps[rows, bank(1 - f)], ones[:, 0:D], e, start=t == PE_TILES[0], stop=t == PE_TILES[-1])
                    m.then_inc(pv_done, 1)

                def denominators(n, f):
                    pe.wait_ge(v_sum, (2 * n + f + 1) * VH)
                    pe.wait_ge(att_copied, 2 * n + f + 1)
                    for t in range(TW):
                        tok = slice(t * P, (t + 1) * P)
                        pe.matmul(ps[:, bank(f), HALF * t:HALF * (t + 1)], pesums[:, tok], sel[:], start=True, stop=False)
                        for j in range(HALF):
                            m = pe.matmul(ps[:, bank(f), HALF * t + j:HALF * t + j + 1], sums[:, f, j, tok], ones[:, 0:1], start=False, stop=j == HALF - 1)
                    m.then_inc(den_ps, 1)

                def turn(n, f):
                    pe.wait_ge(den_rec, 2 * n + f + 1)
                    for t in range(TW):
                        m = pe.transpose(ps[:, bank(f), t * P:(t + 1) * P], att[:, t * P:(t + 1) * P], ident[:])
                    m.then_inc(att_t, 1)

                def project(n, h):
                    if h == 0:
                        pe.wait_ge(att_ready, TW * (2 * n + 2))
                        pe.wait_ge(x_in, 16 * (n + 1))
                    else:
                        pe.wait_ge(x1_ready, 2 * n + 1)
                    for tt in range(2):
                        t = 2 * h + tt
                        for f in range(2):
                            pe.matmul(ps[:, bank(1), tt * C:(tt + 1) * C], O[:, 2 * h + f, tt].rearrange("p j d -> p (j d)"), wpt[:, f, :], start=f == 0, stop=False)
                        for k in range(CK):
                            m = pe.matmul(ps[:, bank(1), tt * C + k * P:tt * C + (k + 1) * P], xres[:, k, t * P:(t + 1) * P],
                                          ident[:], start=False, stop=k == CK - 1)
                    m.then_inc(proj_ps, 1)

                def leftovers(n, i, first):
                    f, g = divmod(i, NG)
                    if first and f == 0:
                        return
                    pn, pf = (n, 0) if f else (n - 1, 1)
                    if g == AT_DEN:
                        denominators(pn, pf)
                    if g == AT_TURN:
                        turn(pn, pf)
                    if g in AT_PROJ and pf:
                        project(pn, AT_PROJ.index(g))

                def chunk(n, first=False):
                    for i in range(N2):
                        pe.wait_ge(expd, n * N2 + i + 1)
                        scores(n, (i + 2) % N2, (i + 2) // N2)
                        values(n, i, first)
                        leftovers(n, i, first)

                scores(0, 0)
                scores(0, 1)
                chunk(0, first=True)
                with pe.Fori(1, NW) as n:
                    chunk(n)
                denominators(NW - 1, 1)
                turn(NW - 1, 1)
                project(NW - 1, 0)
                project(NW - 1, 1)

            @block.scalar
            def _(s):
                def x1_copy(n, h):
                    s.wait_ge(proj_ps, 2 * n + h + 1)
                    s.activation(X1[:, bass.ds(n * TW + 2 * h, 2), :], ps[:, bank(1)].rearrange("p (a c) -> p a c", a=2), ACT.Copy).then_inc(x1_ready, 1)

                def chunk(n, first=False):
                    for i in range(N2):
                        g, u = i % NG, last_user(i)
                        s.wait_ge(scored, n * N2 + i + 1)
                        if u >= 0 or not first:
                            s.wait_ge(pv_done, n * N2 + u + 1)
                            if VS[u % N2]:
                                s.wait_ge(v_sum, 2 * VH * n + (sum(VS[:u + 1]) if u >= 0 else sum(VS[:u % N2 + 1]) - 2 * VH))
                        nb = len(groups[g])
                        s.activation(Pb[:, slots[i], 0:nb], ps[:, 3 * (i % 2):3 * (i % 2) + nb], ACT.Exp).then_inc(expd, 1)
                        if i < NG and g in AT_X1 and not first:
                            x1_copy(n - 1, AT_X1.index(g))

                chunk(0, first=True)
                with s.Fori(1, NW) as n:
                    chunk(n)
                x1_copy(NW - 1, 0)
                x1_copy(NW - 1, 1)

            @block.vector
            def _(v):
                def take(n, f, first=False):
                    v.wait_ge(pv_done, (2 * n + f + 1) * NG)
                    if not first:
                        v.wait_ge(att_t, 2 * n + f)
                    v.tensor_copy(att[:], ps[:, bank(f)]).then_inc(att_copied, 1)

                def invert(n, f):
                    v.wait_ge(den_ps, 2 * n + f + 1)
                    v.reciprocal(rden[:], ps[:, bank(f), 0:TW * HALF].rearrange("p (t j a) -> p t j a", t=TW, j=HALF)).then_inc(den_rec, 1)

                def normalise(n, f, first=False):
                    v.wait_ge(den_rec, 2 * n + f + 1)
                    v.wait_ge(att_t, 2 * n + f + 1)
                    if not first and f == 0:
                        v.wait_ge(proj_ps, 2 * n)
                    for t in range(TW):
                        v.tensor_tensor(O[:, t, f], ps[:, bank(f), t * P:(t + 1) * P].rearrange("p (j d) -> p j d", j=HALF),
                                        rden[:, t].broadcast_to([P, HALF, D]), ALU.mult).then_inc(att_ready, 1)

                def chunk(n, first=False):
                    for i in range(N2):
                        f, g = divmod(i, NG)
                        if not (first and f == 0):
                            pn, pf = (n, 0) if f else (n - 1, 1)
                            if g == 0:
                                take(pn, pf, first)
                            if g == AT_DEN + 1:
                                invert(pn, pf)
                            if g == AT_TURN + 1:
                                normalise(pn, pf, first)
                        if g == AT_SUMS:
                            v.wait_ge(pv_done, n * N2 + f * NG + max(k for k in range(NG) if any(t == PE_TILES[-1] for t, j in groups[k])) + 1)
                            if not (first and f == 0):
                                v.wait_ge(den_ps, 2 * n + f)
                            v.tensor_copy(pesums[:], ps[:, bank(1 - f)]).then_inc(pesum_copied, 1)
                        if VS[i]:
                            v.wait_ge(expd, n * N2 + i + 1)
                        if g == 0 and not first:
                            v.wait_ge(den_ps, 2 * n + f - 1)
                        base = n * 2 * VH + sum(VS[:i])
                        for k, (b, m, j, new) in enumerate(adds(g)):
                            src = Pb[:, slots[i], b:b + m]
                            if new:
                                v.tensor_copy(sums[:, f, j:j + m], src).then_inc(v_sum, 1)
                            else:
                                v.wait_ge(v_sum, base + k)
                                v.tensor_tensor(sums[:, f, j:j + m], sums[:, f, j:j + m], src, ALU.add).then_inc(v_sum, 1)

                chunk(0, first=True)
                with v.Fori(1, NW) as n:
                    chunk(n)
                take(NW - 1, 1)
                invert(NW - 1, 1)
                normalise(NW - 1, 1)

            @block.gpsimd
            def _(g):
                g.memset(zeros[:], 0.0).then_inc(zeroed, 1)


def phase_c(nc, sb, sem, ps, ident, rwt, X1, w1, w2, w3, sorted_x, sorted_y, out_v):
    with ExitStack() as c:
        gate = sb("gate", [P, 2, NT], F32, c)
        slot = sb("slot", [P, 2, NT], I32, c)
        expert = sb("expert", [1, NTS], I32, c)
        W1 = sb("W1", [P, E, CK, H], F32, c)
        W3 = sb("W3", [P, E, CK, H], F32, c)
        W2 = sb("W2", [P, E, HC, C], F32, c)
        route(nc, sb, sem, ps, ident, rwt, X1, gate, slot, expert, W1, W2, W3, w1, w2, w3, sorted_x)
        experts(nc, sb, sem, ps, ident, expert, W1, W2, W3, sorted_x, sorted_y)
        combine(nc, sb, sem, ps, ident, X1, gate, slot, sorted_y, out_v)


def route(nc, sb, sem, ps, ident, rwt, X1, gate, slot, expert, W1, W2, W3, w1, w2, w3, sorted_x):
    with ExitStack() as c:
        XH = sb("XH", [P, NT, C], F32, c)
        st = sb("st", [P, NT, 6], F32, c)
        mv = sb("mv", [P, NT, 2], F32, c)
        rs = sb("rs", [P, NT, 1], F32, c)
        xt = sb("xt", [P, CK, P], F32, c)
        lg = sb("lg", [P, NT, E], F32, c)
        pr = sb("pr", [P, NT, E], F32, c)
        best = sb("best", [P, NT, 1], F32, c)
        best2 = sb("best2", [P, NT, 1], F32, c)
        top = sb("top", [P, NT, 1], F32, c)
        rev = sb("rev", [P, E], F32, c)
        revi = sb("revi", [P, E], I32, c)
        tile_no = sb("tile_no", [1, NTS], F32, c)
        ended = sb("ended", [1, NTS], F32, c)
        tile_noi = sb("tile_noi", [1, NTS], I32, c)
        tmp = lg
        oh = [sb(f"oh{i}", [P, NT, E], F32, c) for i in range(2)]
        cnt = [pr, tmp]
        before = sb("before", [P, P], F32, c)
        ones = sb("ones_c", [P, P], F32, c)
        tiles_f = sb("tiles_f", [P, 3, E], F32, c)
        tiles_i = sb("tiles_i", [P, E], I32, c)
        epst = sb("epst", [P, 1], F32, c)
        w_in, cst, stat, aggr, var_r, std_r, xn, t_ps, t_cp, l_ps, l_cp, ex, mx, ch, masks, ranks, slots, sent = [sem("r_" + n, c) for n in (
            "w_in", "cst", "stat", "aggr", "var", "std", "xn", "t_ps", "t_cp", "l_ps", "l_cp", "ex", "mx", "ch", "masks", "ranks", "slots", "sent")]
        B3 = [P, NT, E]
        TP, LG, RK, TOT = 7, 6, 5, 4
        w1_v = w1.rearrange("(k p) e h -> p e k h", p=P)
        w3_v = w3.rearrange("(k p) e h -> p e k h", p=P)
        with nc.Block() as block:
            @block.sync
            def _(sp):
                for e in range(E):
                    sp.dma_start(W1[:, e], w1_v[:, e]).then_inc(w_in, 16)
                    sp.dma_start(W3[:, e], w3_v[:, e]).then_inc(w_in, 16)
                    sp.dma_start(W2[:, e, 0:HC - 1, :], w2[e, 0:(HC - 1) * P, :].rearrange("(k p) c -> p k c", p=P)).then_inc(w_in, 16)
                    sp.dma_start(W2[0:HL, e, HC - 1, :], w2[e, (HC - 1) * P:H, :]).then_inc(w_in, 16)
                sp.wait_ge(w_in, 16 * 4 * E)

            @block.gpsimd
            def _(g):
                g.iota(revi[:], pattern=[[-1, E]], base=E, channel_multiplier=0).then_inc(cst, 1)
                g.memset(epst[:], EPS_T).then_inc(cst, 1)
                g.memset(ones[:], 1.0).then_inc(cst, 1)
                g.memset(before[:], 0.0).then_inc(cst, 1)
                g.wait_ge(cst, 4)
                g.affine_select(out=before[:], in_=before[:], compare_op=ALU.is_ge, fill=1.0, base=0,
                                pattern=[[-1, P]], channel_multiplier=1).then_inc(cst, 1)
                g.wait_ge(cst, 5)
                g.iota(tile_noi[:], pattern=[[1, NTS]], base=0, channel_multiplier=0).then_inc(cst, 1)
                g.wait_ge(slots, 1)
                for t in range(NT):
                    for i in range(2):
                        g.indirect_dma_start(sorted_x[:, :], bass.IndirectOffsetOnAxis(slot[:, i, t:t + 1], 0), XH[:, t, :], None).then_inc(sent, 16)
                g.wait_ge(sent, 16 * 2 * NT)

            @block.vector
            def _(v):
                n_ch = [0]

                def chain(ins):
                    n_ch[0] += 1
                    ins.then_inc(ch, 1)
                    v.wait_ge(ch, n_ch[0])

                for t in range(NT):
                    v.bn_stats(st[:, t], X1[:, t, :]).then_inc(stat, 1)
                for t in range(NT):
                    v.wait_ge(stat, t + 1)
                    v.bn_aggr(mv[:, t, :], st[:, t]).then_inc(aggr, 1)
                v.wait_ge(aggr, NT)
                v.tensor_copy(best[:, :, 0], mv[:, :, 0]).then_inc(var_r, 1)
                v.wait_ge(std_r, 1)
                chain(v.reciprocal(rs[:], rs[:]))
                v.wait_ge(var_r, 1)
                for t in range(NT):
                    v.tensor_scalar(XH[:, t], X1[:, t], best[:, t], rs[:, t], ALU.subtract, ALU.mult).then_inc(xn, 1)
                with v.Fori(0, NT) as t:
                    v.wait_ge(t_ps, t + 1)
                    v.tensor_copy(xt[:], ps[:, TP, 0:C].rearrange("p (k m) -> p k m", k=CK)).then_inc(t_cp, 1)
                    v.wait_ge(l_ps, t + 1)
                    v.tensor_copy(lg[:, bass.ds(t, 1), :], ps[:, LG:LG + 1, 0:E]).then_inc(l_cp, 1)
                v.wait_ge(l_cp, NT)
                chain(v.tensor_reduce(best[:, :, 0], lg[:], X, ALU.max))
                v.tensor_tensor(lg[:], lg[:], best[:].broadcast_to(B3), ALU.subtract).then_inc(mx, 1)
                v.wait_ge(ex, 1)
                chain(v.tensor_reduce(best[:, :, 0], pr[:], X, ALU.add))
                chain(v.reciprocal(best[:], best[:]))
                chain(v.tensor_tensor(pr[:], pr[:], best[:].broadcast_to(B3), ALU.mult))
                v.wait_ge(cst, 6)
                chain(v.tensor_copy(rev[:], revi[:]))
                rev_b = rev[:].rearrange("p (a e) -> p a e", a=1).broadcast_to(B3)

                def pick(val, mask, probs):
                    chain(v.tensor_reduce(val[:, :, 0], probs[:], X, ALU.max))
                    chain(v.tensor_tensor(mask[:], probs[:], val[:].broadcast_to(B3), ALU.is_equal))
                    chain(v.tensor_tensor(mask[:], mask[:], rev_b, ALU.mult))
                    chain(v.tensor_reduce(top[:, :, 0], mask[:], X, ALU.max))
                    chain(v.tensor_tensor(mask[:], mask[:], top[:].broadcast_to(B3), ALU.is_equal))

                pick(best, oh[0], pr)
                chain(v.tensor_scalar(tmp[:], oh[0][:], -1.0, 1.0, ALU.mult, ALU.add))
                chain(v.tensor_tensor(tmp[:], tmp[:], pr[:], ALU.mult))
                chain(v.tensor_tensor(tmp[:], tmp[:], oh[0][:], ALU.subtract))
                pick(best2, oh[1], tmp)
                v.tensor_tensor(tmp[:], oh[0][:], oh[1][:], ALU.add).then_inc(masks, 1)
                chain(v.tensor_tensor(top[:], best[:], best2[:], ALU.add))
                chain(v.tensor_scalar(top[:], top[:], 1e-9, None, ALU.add))
                chain(v.reciprocal(top[:], top[:]))
                v.tensor_tensor(gate[:, 0], best[:, :, 0], top[:, :, 0], ALU.mult).then_inc(aggr, 1)
                v.tensor_tensor(gate[:, 1], best2[:, :, 0], top[:, :, 0], ALU.mult).then_inc(aggr, 1)
                v.wait_ge(ranks, 1)
                tot = ps[:, TOT, 0:NT * E].rearrange("p (t e) -> p t e", t=NT)
                chain(v.tensor_copy(cnt[0][:], tot))
                cur, d = 0, 1
                while d < NT:
                    a, b = cnt[cur], cnt[1 - cur]
                    chain(v.tensor_copy(b[:, 0:d], a[:, 0:d]))
                    chain(v.tensor_tensor(b[:, d:NT], a[:, d:NT], a[:, 0:NT - d], ALU.add))
                    cur, d = 1 - cur, 2 * d
                total = cnt[cur]
                chain(v.tensor_scalar(tiles_f[:, 0], total[:, NT - 1], float(P - 1), None, ALU.add))
                chain(v.tensor_copy(tiles_i[:], tiles_f[:, 0]))
                chain(v.tensor_scalar(tiles_i[:], tiles_i[:], P.bit_length() - 1, None, ALU.logical_shift_right))
                chain(v.tensor_copy(tiles_f[:, 0], tiles_i[:]))
                src, d = 0, 1
                while d < E:
                    chain(v.tensor_copy(tiles_f[:, 1 - src, 0:d], tiles_f[:, src, 0:d]))
                    chain(v.tensor_tensor(tiles_f[:, 1 - src, d:E], tiles_f[:, src, d:E], tiles_f[:, src, 0:E - d], ALU.add))
                    src, d = 1 - src, 2 * d
                ends, base = tiles_f[:, src], tiles_f[:, 1 - src]
                chain(v.tensor_copy(tile_no[:], tile_noi[:]))
                chain(v.memset(ended[:], 0.0))
                for e in range(E):
                    chain(v.scalar_tensor_tensor(ended[:], tile_no[:], ends[0:1, e:e + 1], ended[:], ALU.is_ge, ALU.add))
                v.tensor_scalar(expert[:], ended[:], float(E - 1), None, ALU.min).then_inc(aggr, 1)
                chain(v.tensor_copy(tiles_f[:, 2], tiles_i[:]))
                chain(v.tensor_tensor(base, ends, tiles_f[:, 2], ALU.subtract))
                chain(v.tensor_scalar(base, base, float(P), None, ALU.mult))
                other = cnt[1 - cur]
                chain(v.tensor_tensor(other[:], total[:], tot, ALU.subtract))
                chain(v.tensor_tensor(other[:], other[:], ps[:, RK, 0:NT * E].rearrange("p (t e) -> p t e", t=NT), ALU.add))
                chain(v.tensor_tensor(other[:], other[:], base.rearrange("p (a e) -> p a e", a=1).broadcast_to(B3), ALU.add))
                for i in range(2):
                    chain(v.tensor_tensor(oh[i][:], oh[i][:], other[:], ALU.mult))
                    chain(v.tensor_reduce(best[:, :, 0], oh[i][:], X, ALU.add))
                    m = v.tensor_copy(slot[:, i], best[:, :, 0])
                    if i == 0:
                        chain(m)
                    else:
                        m.then_inc(slots, 1)

            @block.scalar
            def _(s):
                s.wait_ge(cst, 2)
                s.wait_ge(aggr, NT)
                s.activation(rs[:, :, 0], mv[:, :, 1], ACT.Sqrt, bias=epst[:]).then_inc(std_r, 1)
                s.wait_ge(mx, 1)
                s.activation(pr[:], lg[:], ACT.Exp).then_inc(ex, 1)

            @block.tensor
            def _(pe):
                for t in range(NT):
                    pe.wait_ge(xn, t + 1)
                    if t:
                        pe.wait_ge(l_cp, t)
                    for k in range(CK):
                        m = pe.transpose(ps[:, TP, k * P:(k + 1) * P], XH[:, t, k * P:(k + 1) * P], ident[:])
                    m.then_inc(t_ps, 1)
                    pe.wait_ge(t_cp, t + 1)
                    for k in range(CK):
                        m = pe.matmul(ps[:, LG, 0:E], xt[:, k], rwt[:, k], start=k == 0, stop=k == CK - 1)
                    m.then_inc(l_ps, 1)
                pe.wait_ge(masks, 1)
                pe.wait_ge(cst, 5)
                both = tmp[:].rearrange("p t e -> p (t e)")
                pe.matmul(ps[:, RK, 0:NT * E], before[:], both, start=True, stop=True)
                pe.matmul(ps[:, TOT, 0:NT * E], ones[:], both, start=True, stop=True).then_inc(ranks, 1)


def experts(nc, sb, sem, ps, ident, expert, W1, W2, W3, sorted_x, sorted_y):
    with ExitStack() as c:
        xs = sb("xs", [P, C], F32, c)
        xt = sb("xt2", [P, CK, P], F32, c)
        sg = sb("sg", [P, H], F32, c)
        hh = sb("hh", [P, H], F32, c)
        hT = sb("hT", [P, HC, P], F32, c)
        y = sb("y", [P, C], F32, c)
        x_in, t_ps, t_cp, h1_ps, h3_ps, sg_r, h_r, ht_ps, ht_cp, ht_cs, y_ps, y_cp, y_out = [sem("e_" + n, c) for n in (
            "x_in", "t_ps", "t_cp", "h1_ps", "h3_ps", "sg_r", "h_r", "ht_ps", "ht_cp", "ht_cs", "y_ps", "y_cp", "y_out")]
        A1, A3, AT, AY, AX = 0, 2, 4, 6, 7
        halves = [(0, W), (W, H)]
        rows = [P] * (HC - 1) + [HL]
        with nc.Block() as block:
            @block.sync
            def _(sp):
                sp.dma_start(xs[:], sorted_x[0:P, :]).then_inc(x_in, 16)
                for i in range(2):
                    sp.wait_ge(t_ps, i + 1)
                    sp.dma_start(xs[:], sorted_x[(i + 1) * P:(i + 2) * P, :]).then_inc(x_in, 16)
                with sp.Fori(2, NTS) as i:
                    following, turned, copied, at = sp.snap((i + 1) * P), sp.snap(i + 1), sp.snap(i - 1), sp.snap((i - 2) * P)
                    sp.wait_ge(t_ps, turned)
                    sp.dma_start(xs[:], sorted_x[bass.ds(following, P), :]).then_inc(x_in, 16)
                    sp.wait_ge(y_cp, copied)
                    sp.dma_start(sorted_y[bass.ds(at, P), :], y[:]).then_inc(y_out, 16)
                for i in (NTS - 2, NTS - 1):
                    sp.wait_ge(y_cp, i + 1)
                    sp.dma_start(sorted_y[i * P:(i + 1) * P, :], y[:]).then_inc(y_out, 16)
                sp.wait_ge(y_out, 16 * NTS)
                sp.wait_ge(x_in, 16 * (NTS + 1))

            @block.tensor
            def _(pe):
                def turn_x(i):
                    pe.wait_ge(x_in, 16 * (i + 1))
                    for k in range(CK):
                        m = pe.transpose(ps[:, AX, k * P:(k + 1) * P], xs[:, k * P:(k + 1) * P], ident[:])
                    m.then_inc(t_ps, 1)

                def expand(w, bank, e, done):
                    for n, (a, b) in enumerate(halves):
                        for k in range(CK):
                            m = pe.matmul(ps[:, bank + n, 0:b - a], xt[:, k], w[:, bass.ds(e, 1), k, a:b].rearrange("p a h -> p (a h)"), start=k == 0, stop=k == CK - 1)
                    m.then_inc(done, 1)

                def turn_h(i):
                    pe.wait_ge(h_r, 2 * (i + 1))
                    for k in range(HC):
                        m = pe.transpose(ps[0:rows[k], AT + k // 4, (k % 4) * P:(k % 4 + 1) * P], hh[:, k * P:k * P + rows[k]], ident[:])
                    m.then_inc(ht_ps, 1)

                def shrink(i, e):
                    pe.wait_ge(ht_cp, 2 * (i + 1))
                    pe.wait_ge(ht_cs, i + 1)
                    for k in range(HC):
                        m = pe.matmul(ps[:, AY, 0:C], hT[0:rows[k], k], W2[0:rows[k], bass.ds(e, 1), k, :].rearrange("p a c -> p (a c)"), start=k == 0, stop=k == HC - 1)
                    m.then_inc(y_ps, 1)

                def load_expert(i):
                    return pe.value_load(expert[0:1, bass.ds(i, 1)], min_val=0, max_val=E - 1)

                turn_x(0)
                pe.wait_ge(t_cp, 1)
                e0 = load_expert(0)
                expand(W1, A1, e0, h1_ps)
                expand(W3, A3, e0, h3_ps)
                turn_x(1)
                with pe.Fori(1, NTS) as i:
                    e = load_expert(i)
                    pe.wait_ge(t_cp, i + 1)
                    pe.wait_ge(sg_r, i)
                    expand(W1, A1, e, h1_ps)
                    turn_h(i - 1)
                    expand(W3, A3, e, h3_ps)
                    turn_x(i + 1)
                    shrink(i - 1, load_expert(i - 1))
                turn_h(NTS - 1)
                shrink(NTS - 1, load_expert(NTS - 1))

            @block.scalar
            def _(s):
                def silu(i):
                    s.wait_ge(h1_ps, i + 1)
                    for n, (a, b) in enumerate(halves):
                        m = s.activation(sg[:, a:b], ps[:, A1 + n, 0:b - a], ACT.Silu)
                    m.then_inc(sg_r, 1)

                def turned(i):
                    s.wait_ge(ht_ps, i + 1)
                    s.activation(hT[:, 0:4], ps[:, AT].rearrange("p (k m) -> p k m", k=4), ACT.Copy).then_inc(ht_cs, 1)

                silu(0)
                with s.Fori(1, NTS) as i:
                    s.wait_ge(h_r, 2 * i)
                    silu(i)
                    turned(i - 1)
                turned(NTS - 1)

            @block.vector
            def _(v):
                def x_copy(i):
                    v.wait_ge(t_ps, i + 1)
                    v.tensor_copy(xt[:], ps[:, AX, 0:C].rearrange("p (k m) -> p k m", k=CK)).then_inc(t_cp, 1)

                def gated(i):
                    v.wait_ge(sg_r, i + 1)
                    v.wait_ge(h3_ps, i + 1)
                    for n, (a, b) in enumerate(halves):
                        v.tensor_tensor(hh[:, a:b], sg[:, a:b], ps[:, A3 + n, 0:b - a], ALU.mult).then_inc(h_r, 1)

                def turned(i):
                    v.wait_ge(ht_ps, i + 1)
                    v.tensor_copy(hT[:, 4], ps[:, AT + 1, 0:P]).then_inc(ht_cp, 1)
                    v.tensor_copy(hT[0:HL, 5], ps[0:HL, AT + 1, P:2 * P]).then_inc(ht_cp, 1)

                def y_copy(i, first=False):
                    v.wait_ge(y_ps, i + 1)
                    if not first:
                        v.wait_ge(y_out, 16 * i)
                    v.tensor_copy(y[:], ps[:, AY, 0:C]).then_inc(y_cp, 1)

                x_copy(0)
                gated(0)
                v.wait_ge(h3_ps, 1)
                x_copy(1)
                v.wait_ge(ht_ps, 1)
                turned(0)
                v.wait_ge(h3_ps, 2)
                gated(1)
                x_copy(2)
                y_copy(0, first=True)
                with v.Fori(2, NTS) as i:
                    turned(i - 1)
                    gated(i)
                    x_copy(i + 1)
                    y_copy(i - 1)
                turned(NTS - 1)
                y_copy(NTS - 1)


def combine(nc, sb, sem, ps, ident, X1, gate, slot, sorted_y, out_v):
    NB = 4
    with ExitStack() as c:
        Y = sb("Y", [P, NB, 2, C], F32, c)
        fin = sb("fin", [P, 2, C], F32, c)
        fo = sb("fo", [P, 2, CK, P], F32, c)
        y_in = [sem(f"y_in{b}", c) for b in range(NB)]
        part, fin_r, o_ps, o_cp = [sem("f_" + n, c) for n in ("part", "fin_r", "o_ps", "o_cp")]
        o_out = [sem(f"o_out{b}", c) for b in range(2)]
        with nc.Block() as block:
            @block.gpsimd
            def _(g):
                for t in range(NT):
                    if t >= NB:
                        g.wait_ge(fin_r, t - NB + 1)
                    for i in range(2):
                        g.indirect_dma_start(Y[:, t % NB, i, :], None, sorted_y[:, :], bass.IndirectOffsetOnAxis(slot[:, i, t:t + 1], 0)).then_inc(y_in[t % NB], 16)

            @block.vector
            def _(v):
                for t in range(NT):
                    v.wait_ge(y_in[t % NB], 32 * (t // NB + 1))
                    if t >= 2:
                        v.wait_ge(o_ps, t - 1)
                    v.scalar_tensor_tensor(fin[:, t % 2], Y[:, t % NB, 0], gate[:, 0, t:t + 1], X1[:, t], ALU.mult, ALU.add).then_inc(part, 1)
                    v.wait_ge(part, t + 1)
                    v.scalar_tensor_tensor(fin[:, t % 2], Y[:, t % NB, 1], gate[:, 1, t:t + 1], fin[:, t % 2], ALU.mult, ALU.add).then_inc(fin_r, 1)

            @block.tensor
            def _(pe):
                for t in range(NT):
                    pe.wait_ge(fin_r, t + 1)
                    if t >= 2:
                        pe.wait_ge(o_cp, t - 1)
                    for k in range(CK):
                        m = pe.transpose(ps[:, t % 2, k * P:(k + 1) * P], fin[:, t % 2, k * P:(k + 1) * P], ident[:])
                    m.then_inc(o_ps, 1)

            @block.scalar
            def _(s):
                for t in range(NT):
                    s.wait_ge(o_ps, t + 1)
                    if t >= 2:
                        s.wait_ge(o_out[t % 2], 16 * (t // 2))
                    s.activation(fo[:, t % 2], ps[:, t % 2, 0:C].rearrange("p (k m) -> p k m", k=CK), ACT.Copy).then_inc(o_cp, 1)

            @block.sync
            def _(sp):
                for t in range(NT):
                    sp.wait_ge(o_cp, t + 1)
                    sp.dma_start(out_v[:, :, t * P:(t + 1) * P], fo[:, t % 2]).then_inc(o_out[t % 2], 16)
                for b in range(2):
                    sp.wait_ge(o_out[b], 16 * (NT // 2))


def kernel(**inputs):
    import numpy as np
    import concourse.bacc as bacc
    from concourse.bass_utils import run_bass_kernel_spmd

    laid = {
        "x": inputs["x"],
        "wqkv": np.transpose(inputs["L0_conv_w_qkv"]),
        "wproj": np.transpose(inputs["L0_conv_w_proj"]),
        "temp": inputs["L0_conv_temperature"],
        "rw": np.transpose(inputs["L0_ffn_router_w"]),
        "w1": np.transpose(inputs["L0_ffn_w1"], (2, 0, 1)),
        "w2": np.transpose(inputs["L0_ffn_w2"], (0, 2, 1)),
        "w3": np.transpose(inputs["L0_ffn_w3"], (2, 0, 1)),
    }
    nc = bacc.Bacc("TRN2", target_bir_lowering=False, num_devices=1)
    arrays, args = {}, []
    for name, a in laid.items():
        a = np.ascontiguousarray(a)
        arrays[f"in_{name}"] = a
        args.append(nc.dram_tensor(f"in_{name}", a.shape, mybir.dt.from_np(a.dtype), kind="ExternalInput").ap())
    args.append(nc.dram_tensor("result", (1, C, 64, 64), F32, kind="ExternalOutput").ap())
    build(nc, *args)
    r = run_bass_kernel_spmd(nc, [arrays], core_ids=[0])
    return r.results[0]["result"]
```

```python
from contextlib import ExitStack

import concourse.bass as bass
from concourse import mybir

F32, F16, I32 = mybir.dt.float32, mybir.dt.float16, mybir.dt.int32
ACT = mybir.ActivationFunctionType
ALU = mybir.AluOpType
X = mybir.AxisListType.X

P = 128
C = 256
S = 4096
NH, D = 8, 32
CK = C // P
HALF = 4
W = 512
NW = S // W
NT = S // P
TW = W // P
E, H = 8, 682
HC = (H + P - 1) // P
HL = H - (HC - 1) * P
KR = 3 * D + 2
NTS = (2 * S + E * (P - 1)) // P
NA = NTS + 1
NY = 1 + 2 * S + NA * P
EPS_C, EPS_T, EPS_N = 1e-6, 1e-5, 1e-12
AHEAD = 2
XSCALE = 16.0
LO, HI = range(2)
R = S // C
RW = W // C


def group_plan():
    units = [(t, j) for t in range(NT) for j in range(HALF)]
    return [units[i:i + 3] for i in range(0, len(units), 3)]


def build(nc, x, wqkv, wproj, temp, rw, w1, w2, w3, out):
    x_v = x.rearrange("a (k p) h w -> p (a k) (h w)", p=P)
    out_v = out.rearrange("a (k p) h w -> p (a k) (h w)", p=P)
    normed = nc.dram_tensor("normed", (S, C), F32, kind="Internal").ap()
    expert_out = nc.dram_tensor("expert_out", (NY, C), F32, kind="Internal").ap()
    with ExitStack() as ctx:
        def sb(name, shape, dt, c=ctx):
            return c.enter_context(nc.sbuf_tensor(name, shape, dt))

        def sem(name, c=ctx):
            return c.enter_context(nc.semaphore(name))

        ident = sb("ident", [P, P], F32)
        rwt = sb("rwt", [P, CK, E], F32)
        X1 = sb("X1", [P, NT, C], F32)
        st = sb("st", [P, NT, 6], F32)
        mv = sb("mv", [P, NT, 2], F32)
        ps = ctx.enter_context(nc.psum_tensor("ps", [P, 8, W], F32))

        with ExitStack() as ab:
            K8 = sb("K8", [P, NH, S], F16, ab)
            V = sb("V", [P, NT, C], F32, ab)
            Q8 = sb("Q8", [P, 2, HALF, W], F16, ab)
            QS = X1[:].rearrange("p t c -> p (t c)").bitcast(F16).rearrange("p (n a k w) -> p n a k w", n=NW, a=2, k=CK)
            wpt = sb("wpt", [P, CK, C], F32, ab)
            ones = sb("ones", [P, P], F32, ab)
            sel = sb("sel", [P, HALF], F32, ab)
            shh = sb("shh", [P, NH, 2], F16, ab)
            q_first = sem("q_first", ab)
            phase_a(nc, ab, sb, sem, ps, x_v, wqkv, wproj, temp, rw, ident, ones, sel, rwt, wpt, K8, V, QS, shh, Q8, X1, q_first)
            phase_b(nc, sb, sem, ps, x_v, ident, ones, sel, wpt, K8, V, QS, Q8, X1, st, mv, q_first)
        phase_c(nc, sb, sem, ps, ident, rwt, X1, st, mv, w1, w2, w3, normed, expert_out, out_v)


def phase_a(nc, ab, sb, sem, ps, x_v, wqkv, wproj, temp, rw, ident, ones, sel, rwt, wpt, K8, V, QS, shh, Q8, X1, q_first):
    with ExitStack() as c:
        xin = sb("xin", [P, CK, W], F32, c)
        xc = sb("xc", [P, 2, CK, W], F32, c)
        xsq = sb("xsq", [P, CK, W], F32, c)
        qraw = sb("qraw", [P, 2 * CK, W], F32, c)
        qsq = sb("qsq", [P, 2 * CK, W], F32, c)
        nrm = sb("nrm", [P, W], F32, c)
        std = sb("std", [P, W], F32, c)
        rn = sb("rn", [P, W], F32, c)
        stdt = sb("stdt", [P, TW], F32, c)
        rt = sb("rt", [P, 2, TW], F32, c)
        wq = sb("wq", [P, CK, 3 * C], F32, c)
        mean_w = sb("mean_w", [P, P], F32, c)
        grp = sb("grp", [P, D], F32, c)
        back = sb("back", [P, HALF, D], F32, c)
        kl = sb("kl", [P, 2, CK, W], F16, c)
        trow = sb("trow", [P, NH], F32, c)
        tneg = sb("tneg", [P, NH], F32, c)
        scale = sb("scale", [P, 2 * CK, 1], F32, c)
        epsc = sb("epsc", [P, 1], F32, c)

        x_in, w_in, const_ready, shift_ready, scale_ready = [sem(n, c) for n in ("x_in", "w_in", "const_ready", "shift_ready", "scale_ready")]
        mean_ps, centred, squared, var_ps, std_ready, stdt_ready, rt_ready = [sem(n, c) for n in (
            "mean_ps", "centred", "squared", "var_ps", "std_ready", "stdt_ready", "rt_ready")]
        qk_ps, q_copied, q_sq, n_ps, n_sqrt, clamped, rn_ready, back_ps = [sem(n, c) for n in (
            "qk_ps", "q_copied", "q_sq", "n_ps", "n_sqrt", "clamped", "rn_ready", "back_ps")]
        q_norm, hi_ready, split_ready, v_ps, v_ready, laid = [sem(n, c) for n in ("q_norm", "hi_ready", "split_ready", "v_ps", "v_ready", "laid")]
        LN, NRM, QK, BACK = 0, 1, 2, 4
        OC = 2 * CK
        CONSTS = 7 + 2 + HALF + HALF

        def rounds(eng, chunk):
            chunk(0, 0, first=True)
            with eng.Fori(1, NW - 1, 2) as n:
                chunk(n, 1)
                chunk(n + 1, 0)
            chunk(NW - 1, 1, last=True)

        with nc.Block() as block:
            @block.sync
            def _(sp):
                def load_x(at):
                    sp.dma_start(xin[:], x_v[:, :, bass.ds(at, W)]).then_inc(x_in, 16)

                def lay(at):
                    for r, a in enumerate((HI, HI, LO)):
                        for j in range(HALF):
                            sp.dma_start(K8[r * D:(r + 1) * D, j:NH:HALF, bass.ds(at, W)],
                                         kl[j * D:(j + 1) * D, a, :, :]).then_inc(laid, 16)

                load_x(0)
                sp.dma_start(trow[:], temp[:, :, 0].rearrange("h a -> a h").broadcast_to([P, NH])).then_inc(w_in, 16)
                sp.dma_start(wq[:], wqkv.rearrange("(k p) o -> p k o", p=P)).then_inc(w_in, 16)
                sp.dma_start(wpt[:], wproj.rearrange("(k p) o -> p k o", p=P)).then_inc(w_in, 16)
                sp.dma_start(rwt[:], rw.rearrange("(k p) o -> p k o", p=P)).then_inc(w_in, 16)
                sp.wait_ge(centred, CK)
                load_x(W)
                sp.wait_ge(centred, 2 * CK)
                load_x(2 * W)
                with sp.Fori(1, NW - 2) as n:
                    before, after, split, read = sp.snap((n - 1) * W), sp.snap((n + 2) * W), sp.snap(OC * n), sp.snap(CK * (n + 2))
                    sp.wait_ge(split_ready, split)
                    lay(before)
                    sp.wait_ge(centred, read)
                    load_x(after)
                for m in range(NW - 3, NW):
                    sp.wait_ge(split_ready, OC * (m + 1))
                    lay(m * W)
                sp.wait_ge(laid, NW * 12 * 16)

            @block.gpsimd
            def _(g):
                g.memset(ident[:], 0.0).then_inc(const_ready, 1)
                g.memset(ones[:], 1.0).then_inc(const_ready, 1)
                g.memset(mean_w[:], 1.0 / C).then_inc(const_ready, 1)
                g.memset(grp[:], 0.0).then_inc(const_ready, 1)
                g.memset(back[:], 0.0).then_inc(const_ready, 1)
                g.memset(epsc[:], EPS_C).then_inc(const_ready, 1)
                g.memset(sel[:], 0.0).then_inc(const_ready, 1)
                g.wait_ge(const_ready, 7)
                g.affine_select(out=ident[:], in_=ident[:], compare_op=ALU.not_equal, fill=1.0, base=0,
                                pattern=[[-1, P]], channel_multiplier=1).then_inc(const_ready, 1)
                g.affine_select(out=sel[:], in_=sel[:], compare_op=ALU.not_equal, fill=1.0, base=0,
                                pattern=[[-D, HALF]], channel_multiplier=1).then_inc(const_ready, 1)
                for j in range(HALF):
                    a = slice(j * D, (j + 1) * D)
                    g.wait_ge(const_ready, 9 + 2 * j)
                    g.memset(grp[a, j * D // HALF:(j + 1) * D // HALF], 1.0).then_inc(const_ready, 1)
                    g.wait_ge(const_ready, 10 + 2 * j)
                    g.affine_select(out=back[a], in_=back[a], compare_op=ALU.not_equal, fill=1.0, base=0,
                                    pattern=[[-D // HALF, HALF], [0, D]], channel_multiplier=1).then_inc(const_ready, 1)
                g.wait_ge(const_ready, CONSTS)
                g.memset(K8[3 * D:3 * D + 2, :, :], 1.0).then_inc(const_ready, 1)
                g.wait_ge(const_ready, CONSTS + 1)
                g.wait_ge(split_ready, OC * NW)
                for r, a in enumerate((HI, LO, HI)):
                    for j in range(HALF):
                        g.dma_start(Q8[r * D:(r + 1) * D, 0, j, :], QS[j * D:(j + 1) * D, 0, a, 0, :]).then_inc(q_first, 16)

            @block.vector
            def _(v):
                def centre(n, b):
                    v.wait_ge(mean_ps, n + 1)
                    for k in range(CK):
                        v.tensor_tensor(xc[:, b, k], xin[:, k], ps[:, LN], ALU.subtract).then_inc(centred, 1)

                def inverse_std(n, b):
                    v.wait_ge(stdt_ready, n + 1)
                    v.reciprocal(rt[:, b], stdt[:]).then_inc(rt_ready, 1)

                def finish(n):
                    v.wait_ge(back_ps, n + 1)
                    for o in range(OC):
                        v.scalar_tensor_tensor(qraw[:, o], qraw[:, o], scale[:, o], ps[:, BACK + o], ALU.mult, ALU.mult).then_inc(q_norm, 1)
                    for o in range(OC):
                        if o < CK:
                            src = qraw[:, o].rearrange("p (c n r) -> p n r c", n=NW, r=RW)
                            hi, lo = [QS[:, :, part, o, :].rearrange("p n (r c) -> p n r c", r=RW)[:, :, :, bass.ds(n * (W // R), W // R)]
                                      for part in (HI, LO)]
                        else:
                            if o == CK and not (isinstance(n, int) and n == 0):
                                v.wait_ge(laid, n * 12 * 16)
                            src, hi, lo = qraw[:, o], kl[:, HI, o - CK], kl[:, LO, o - CK]
                        v.wait_ge(q_norm, OC * n + o + 1)
                        v.tensor_copy(hi, src).then_inc(hi_ready, 1)
                        v.wait_ge(hi_ready, OC * n + o + 1)
                        v.tensor_tensor(lo, src, hi, ALU.subtract).then_inc(split_ready, 1)

                def inverse_norms(n):
                    v.wait_ge(n_sqrt, n + 1)
                    v.wait_ge(std_ready, n + 1)
                    v.scalar_tensor_tensor(nrm[:], std[:], EPS_N, nrm[:], ALU.mult, ALU.max).then_inc(clamped, 1)
                    v.wait_ge(clamped, n + 1)
                    v.reciprocal(rn[:], nrm[:]).then_inc(rn_ready, 1)

                def chunk(n, b, first=False, last=False):
                    if not first:
                        finish(n - 1)
                    if not last:
                        centre(n + 1, 1 - b)
                    inverse_norms(n)
                    if not last:
                        inverse_std(n + 1, 1 - b)

                v.wait_ge(const_ready, CONSTS)
                v.wait_ge(w_in, 16 * 4)
                centre(0, 0)
                v.memset(scale[:, CK:OC, :], 1.0).then_inc(scale_ready, 1)
                for j in range(HALF):
                    a = slice(j * D, (j + 1) * D)
                    v.tensor_copy(scale[a, 0:CK, 0], trow[a, j:NH:HALF]).then_inc(scale_ready, 1)
                v.tensor_scalar(tneg[:], trow[:], -1.0, None, ALU.mult).then_inc(shift_ready, 1)
                v.wait_ge(shift_ready, 1)
                v.tensor_tensor(tneg[:], trow[:], tneg[:], ALU.min).then_inc(shift_ready, 1)
                v.wait_ge(shift_ready, 2)
                v.tensor_copy(shh[:, :, 0], tneg[:]).then_inc(shift_ready, 1)
                v.wait_ge(shift_ready, 3)
                v.tensor_tensor(shh[:, :, 1], tneg[:], shh[:, :, 0], ALU.subtract).then_inc(shift_ready, 1)
                v.wait_ge(shift_ready, 4)
                for r, rows in ((1, 2), (0, 1)):
                    a = slice(3 * D, 3 * D + rows)
                    v.tensor_copy(Q8[a].rearrange("p f j w -> p (f j) w"), shh[a, :, r:r + 1].broadcast_to([rows, NH, W])).then_inc(shift_ready, 1)
                    v.wait_ge(shift_ready, 6 - r)
                v.wait_ge(scale_ready, 1 + HALF)
                inverse_std(0, 0)
                rounds(v, chunk)
                finish(NW - 1)

            @block.scalar
            def _(s):
                def square_x(n, b):
                    s.wait_ge(centred, CK * (n + 1))
                    s.activation(xsq[:], xc[:, b], ACT.Square).then_inc(squared, 1)

                def stds(n):
                    s.wait_ge(var_ps, n + 1)
                    if not (isinstance(n, int) and n == 0):
                        s.wait_ge(clamped, n)
                        s.wait_ge(rt_ready, n)
                    s.activation(std[:], ps[:, LN], ACT.Sqrt, bias=epsc[:]).then_inc(std_ready, 1)
                    s.activation(stdt[:], ps[:, NRM, 0:TW], ACT.Sqrt, bias=epsc[:]).then_inc(stdt_ready, 1)

                def chunk(n, b, first=False, last=False):
                    for o in range(OC):
                        s.wait_ge(qk_ps, OC * n + o + 1)
                        if not first:
                            s.wait_ge(split_ready, OC * (n - 1) + o + 1)
                        s.activation(qraw[:, o], ps[:, QK + o % 2], ACT.Copy).then_inc(q_copied, 1)
                        s.wait_ge(q_copied, OC * n + o + 1)
                        s.activation(qsq[:, o], qraw[:, o], ACT.Square).then_inc(q_sq, 1)
                    if not last:
                        square_x(n + 1, 1 - b)
                    s.wait_ge(n_ps, n + 1)
                    if not first:
                        s.wait_ge(rn_ready, n)
                    s.activation(nrm[:], ps[:, NRM], ACT.Sqrt).then_inc(n_sqrt, 1)
                    s.wait_ge(rt_ready, n + 1)
                    for t in range(TW):
                        if t % 2 == 0:
                            s.wait_ge(v_ps, 2 * n + t // 2 + 1)
                        s.activation(V[:, bass.ds(n * TW + t, 1), :], ps[:, QK + t // 2, (t % 2) * C:(t % 2 + 1) * C].rearrange("p (a c) -> p a c", a=1),
                                     ACT.Copy, scale=rt[:, b, t:t + 1]).then_inc(v_ready, 1)
                    if not last:
                        stds(n + 1)

                s.wait_ge(const_ready, CONSTS)
                square_x(0, 0)
                stds(0)
                rounds(s, chunk)

            @block.tensor
            def _(pe):
                def mean(n):
                    pe.wait_ge(x_in, 16 * (n + 1))
                    if not (isinstance(n, int) and n == 0):
                        pe.wait_ge(std_ready, n)
                    for k in range(CK):
                        m = pe.matmul(ps[:, LN], mean_w[:], xin[:, k], start=k == 0, stop=k == CK - 1)
                    m.then_inc(mean_ps, 1)

                def variance(n):
                    pe.wait_ge(squared, n + 1)
                    if not (isinstance(n, int) and n == 0):
                        pe.wait_ge(n_sqrt, n)
                    for k in range(CK):
                        pe.matmul(ps[:, LN], mean_w[:], xsq[:, k], start=k == 0, stop=k == CK - 1)
                    for t in range(TW):
                        for k in range(CK):
                            m = pe.matmul(ps[:, NRM, t:t + 1], xsq[:, k, t * P:(t + 1) * P], mean_w[:, 0:1], start=k == 0, stop=k == CK - 1)
                    m.then_inc(var_ps, 1)

                def spread(n):
                    pe.wait_ge(rn_ready, n + 1)
                    for o in range(OC):
                        a = slice(o * D, (o + 1) * D)
                        m = pe.matmul(ps[:, BACK + o], back[a].rearrange("p j d -> p (j d)"), rn[a], start=True, stop=True)
                    m.then_inc(back_ps, 1)

                def chunk(n, b, first=False, last=False):
                    if not first:
                        spread(n - 1)
                    pe.wait_ge(centred, CK * (n + 1))
                    for o in range(OC):
                        if o >= 2:
                            pe.wait_ge(q_copied, OC * n + o - 1)
                        elif not first:
                            pe.wait_ge(v_ready, TW * n - 2 + 2 * o)
                        for k in range(CK):
                            m = pe.matmul(ps[:, QK + o % 2], wq[:, k, o * P:(o + 1) * P], xc[:, b, k], start=k == 0, stop=k == CK - 1)
                        m.then_inc(qk_ps, 1)
                    if not last:
                        mean(n + 1)
                    pe.wait_ge(q_sq, OC * (n + 1))
                    pe.wait_ge(stdt_ready, n + 1)
                    for o in range(OC):
                        m = pe.matmul(ps[o * D:(o + 1) * D, NRM], grp[:], qsq[:, o], start=True, stop=True)
                    m.then_inc(n_ps, 1)
                    for t in range(TW):
                        for k in range(CK):
                            m = pe.matmul(ps[:, QK + t // 2, (t % 2) * C:(t % 2 + 1) * C], xc[:, b, k, t * P:(t + 1) * P], wq[:, k, 2 * C:3 * C],
                                          start=k == 0, stop=k == CK - 1)
                        if t % 2:
                            m.then_inc(v_ps, 1)
                    if not last:
                        variance(n + 1)

                pe.wait_ge(const_ready, CONSTS)
                pe.wait_ge(w_in, 16 * 4)
                mean(0)
                variance(0)
                rounds(pe, chunk)
                spread(NW - 1)


def phase_b(nc, sb, sem, ps, x_v, ident, ones, sel, wpt, K8, V, QS, Q8, X1, st, mv, q_first):
    groups = group_plan()
    NG = len(groups)
    N2 = 2 * NG
    AT_TAKE = 2
    AT_TOTAL, AT_ADD = 4, 5
    AT_DEN, AT_TURN, AT_PROJ, AT_X1, AT_SUMS = 7, 10, (12, 14), (14, 16), 39
    AT_INVERT, AT_NORM = 7, 10
    PE_TILES = (12, 17, 22, 27)
    NP = 5
    short = -N2 % NP
    slots = [k for b in range((N2 + short) // NP) for k in range(NP - (b >= (N2 + short) // NP - short))]
    assert len(slots) == N2

    def last_user(i):
        u = i - 1
        while slots[u % N2] != slots[i]:
            u -= 1
        return u

    def adds(g):
        out = []
        for b, (t, j) in enumerate(groups[g]):
            if t in PE_TILES:
                continue
            if out and out[-1][0] + out[-1][1] == b and out[-1][2] + out[-1][1] == j:
                out[-1][1] += 1
            else:
                out.append([b, 1, j, t == 0])
        return out

    SUMMED = max(g for g in range(NG) if any(t == PE_TILES[-1] for t, j in groups[g])) + 1
    VS = [len(adds(i % NG)) for i in range(N2)]
    VH = sum(VS[:NG])
    spans = [(j, m) for g in range(NG) for b, m, j, new in adds(g)]
    AFTER = [max([k + 1 for k in range(i) if spans[k][0] < j + m and j < spans[k][0] + spans[k][1]], default=0) for i, (j, m) in enumerate(spans)]

    with ExitStack() as c:
        Pb = sb("Pb", [P, NP, 3, W], F32, c)
        sums = sb("sums", [P, 2, HALF, W], F32, c)
        pesums = sb("pesums", [P, W], F32, c)
        att = sb("att", [P, W], F32, c)
        rden = sb("rden", [P, TW, HALF, 1], F32, c)
        O = sb("O", [P, TW, CK, HALF, D], F32, c)
        xres = sb("xres", [P, CK, W], F32, c)

        q_in = [sem(f"q_in{f}", c) for f in range(2)]
        x_in, scored, expd, pv_done, v_sum, pesum_copied, totalled, den_added, den_ps, den_rec, att_copied, att_t, att_ready, proj_ps, x1_ready, stat = [
            sem(n, c) for n in ("xr_in", "scored", "expd", "pv_done", "v_sum", "pesum_copied", "totalled", "den_added", "den_ps", "den_rec", "att_copied", "att_t",
                                "att_ready", "proj_ps", "x1_ready", "stat")]

        def bank(f):
            return 6 + f

        with nc.Block() as block:
            @block.sync
            def _(sp):
                def load_q(n, f):
                    for r, a in enumerate((HI, LO, HI)):
                        for j in range(HALF):
                            sp.dma_start(Q8[r * D:(r + 1) * D, f, j, :],
                                         QS[j * D:(j + 1) * D, bass.ds(n, 1), a, f, :].rearrange("p b w -> p (b w)")).then_inc(q_in[f], 16)

                def load_x(at):
                    sp.dma_start(xres[:], x_v[:, :, bass.ds(at, W)]).then_inc(x_in, 16)

                load_q(0, 1)
                load_x(0)
                with sp.Fori(0, NW - 1) as n:
                    chunk, at, added = sp.snap(n + 1), sp.snap((n + 1) * W), sp.snap(2 * n + 2)
                    read = [sp.snap(N2 * n + (f + 1) * NG) for f in range(2)]
                    for f in range(2):
                        sp.wait_ge(scored, read[f])
                        load_q(chunk, f)
                    sp.wait_ge(proj_ps, added)
                    load_x(at)
                sp.wait_ge(scored, N2 * (NW - 1) + NG)
                load_q(NW - 1, 0)
                sp.wait_ge(x_in, 16 * NW)

            @block.tensor
            def _(pe):
                def scores(n, i, base=0):
                    f, g = divmod(i, NG)
                    if g == 0 and not f and isinstance(n, int) and n + base == 0:
                        pe.wait_ge(q_first, 16 * 3 * HALF)
                    elif g == 0:
                        pe.wait_ge(q_in[f], 16 * 3 * HALF * (n + base + f))
                    for b, (t, j) in enumerate(groups[g]):
                        m = pe.matmul(ps[:, 3 * (i % 2) + b], K8[0:KR, f * HALF + j, t * P:(t + 1) * P], Q8[0:KR, f, j, :], start=True, stop=True)
                    m.then_inc(scored, 1)

                def values(n, i, first):
                    f, g = divmod(i, NG)
                    if g == 0 and not (first and f == 0):
                        pe.wait_ge(pesum_copied, 2 * n + f)
                    for b, (t, j) in enumerate(groups[g]):
                        rows, e = slice(j * D, (j + 1) * D), Pb[:, slots[i], b]
                        if (t, j) == (PE_TILES[0], 0) and f:
                            pe.wait_ge(att_ready, TW * (2 * n + 1))
                        if (t, j) == (PE_TILES[0], 0) and not f and not first:
                            pe.wait_ge(x1_ready, 2 * n)
                        m = pe.matmul(ps[rows, bank(f)], V[:, t, (f * HALF + j) * D:(f * HALF + j + 1) * D], e, start=t == 0, stop=t == NT - 1)
                        if t in PE_TILES:
                            m = pe.matmul(ps[rows, bank(1 - f)], ones[:, 0:D], e, start=t == PE_TILES[0], stop=t == PE_TILES[-1])
                    m.then_inc(pv_done, 1)

                def total(n, f):
                    pe.wait_ge(v_sum, (2 * n + f + 1) * VH)
                    pe.wait_ge(att_copied, 2 * n + f + 1)
                    for j in range(HALF):
                        m = pe.matmul(ps[j * D:(j + 1) * D, bank(f)], ones[:, 0:D], sums[:, f, j], start=True, stop=True)
                    m.then_inc(totalled, 1)

                def denominators(n, f):
                    pe.wait_ge(den_added, 2 * n + f + 1)
                    for t in range(TW):
                        m = pe.matmul(ps[:, bank(f), HALF * t:HALF * (t + 1)], pesums[:, t * P:(t + 1) * P], sel[:], start=True, stop=True)
                    m.then_inc(den_ps, 1)

                def turn(n, f):
                    pe.wait_ge(den_rec, 2 * n + f + 1)
                    for t in range(TW):
                        m = pe.transpose(ps[:, bank(f), t * P:(t + 1) * P], att[:, t * P:(t + 1) * P], ident[:])
                    m.then_inc(att_t, 1)

                def project(n, h):
                    if h == 0:
                        pe.wait_ge(att_ready, TW * (2 * n + 2))
                        pe.wait_ge(x_in, 16 * (n + 1))
                    else:
                        pe.wait_ge(x1_ready, 2 * n + 1)
                    for tt in range(2):
                        t = 2 * h + tt
                        for f in range(2):
                            pe.matmul(ps[:, bank(1), tt * C:(tt + 1) * C], O[:, 2 * h + f, tt].rearrange("p j d -> p (j d)"), wpt[:, f, :], start=f == 0, stop=False)
                        for k in range(CK):
                            m = pe.matmul(ps[:, bank(1), tt * C + k * P:tt * C + (k + 1) * P], xres[:, k, t * P:(t + 1) * P],
                                          ident[:], start=False, stop=k == CK - 1)
                    m.then_inc(proj_ps, 1)

                def leftovers(n, i, first):
                    f, g = divmod(i, NG)
                    if first and f == 0:
                        return
                    pn, pf = (n, 0) if f else (n - 1, 1)
                    if g == AT_TOTAL:
                        total(pn, pf)
                    if g == AT_DEN:
                        denominators(pn, pf)
                    if g == AT_TURN:
                        turn(pn, pf)
                    if g in AT_PROJ and pf:
                        project(pn, AT_PROJ.index(g))

                def chunk(n, first=False):
                    for i in range(N2):
                        pe.wait_ge(expd, n * N2 + i + 1)
                        scores(n, (i + 2) % N2, (i + 2) // N2)
                        values(n, i, first)
                        leftovers(n, i, first)

                scores(0, 0)
                scores(0, 1)
                chunk(0, first=True)
                with pe.Fori(1, NW) as n:
                    chunk(n)
                total(NW - 1, 1)
                denominators(NW - 1, 1)
                turn(NW - 1, 1)
                project(NW - 1, 0)
                project(NW - 1, 1)

            @block.scalar
            def _(s):
                def x1_copy(n, h):
                    s.wait_ge(proj_ps, 2 * n + h + 1)
                    s.activation(X1[:, bass.ds(n * TW + 2 * h, 2), :], ps[:, bank(1)].rearrange("p (a c) -> p a c", a=2), ACT.Copy).then_inc(x1_ready, 1)

                def take(n, f, first=False):
                    s.wait_ge(pv_done, (2 * n + f + 1) * NG)
                    if not first:
                        s.wait_ge(att_t, 2 * n + f)
                    s.activation(att[:], ps[:, bank(f)], ACT.Copy).then_inc(att_copied, 1)

                def take_sums(n, f, first=False):
                    s.wait_ge(pv_done, n * N2 + f * NG + SUMMED)
                    if not first:
                        s.wait_ge(den_ps, 2 * n + f)
                    s.activation(pesums[:], ps[:, bank(1 - f)], ACT.Copy).then_inc(pesum_copied, 1)

                def chunk(n, first=False):
                    for i in range(N2):
                        f = i // NG
                        g, u = i % NG, last_user(i)
                        s.wait_ge(scored, n * N2 + i + 1)
                        if u >= 0 or not first:
                            s.wait_ge(pv_done, n * N2 + u + 1)
                            if VS[u % N2]:
                                s.wait_ge(v_sum, 2 * VH * n + (sum(VS[:u + 1]) if u >= 0 else sum(VS[:u % N2 + 1]) - 2 * VH))
                        nb = len(groups[g])
                        s.activation(Pb[:, slots[i], 0:nb], ps[:, 3 * (i % 2):3 * (i % 2) + nb], ACT.Exp).then_inc(expd, 1)
                        if g == AT_TAKE and f:
                            take(n, 0, first)
                        if g == AT_TAKE and not f and not first:
                            take(n - 1, 1)
                        if g == AT_SUMS:
                            take_sums(n, f, first and not f)
                        if i < NG and g in AT_X1 and not first:
                            x1_copy(n - 1, AT_X1.index(g))

                chunk(0, first=True)
                with s.Fori(1, NW) as n:
                    chunk(n)
                take(NW - 1, 1)
                x1_copy(NW - 1, 0)
                x1_copy(NW - 1, 1)

            @block.vector
            def _(v):
                def add_totals(n, f):
                    v.wait_ge(totalled, 2 * n + f + 1)
                    v.wait_ge(pesum_copied, 2 * n + f + 1)
                    v.tensor_tensor(pesums[:], pesums[:], ps[:, bank(f)], ALU.add).then_inc(den_added, 1)

                def invert(n, f):
                    v.wait_ge(den_ps, 2 * n + f + 1)
                    v.reciprocal(rden[:], ps[:, bank(f), 0:TW * HALF].rearrange("p (t j a) -> p t j a", t=TW, j=HALF)).then_inc(den_rec, 1)

                def normalise(n, f, first=False):
                    v.wait_ge(den_rec, 2 * n + f + 1)
                    v.wait_ge(att_t, 2 * n + f + 1)
                    if not first and f == 0:
                        v.wait_ge(proj_ps, 2 * n)
                    for t in range(TW):
                        v.tensor_tensor(O[:, t, f], ps[:, bank(f), t * P:(t + 1) * P].rearrange("p (j d) -> p j d", j=HALF),
                                        rden[:, t].broadcast_to([P, HALF, D]), ALU.mult).then_inc(att_ready, 1)

                def chunk(n, first=False):
                    for i in range(N2):
                        f, g = divmod(i, NG)
                        if not (first and f == 0):
                            pn, pf = (n, 0) if f else (n - 1, 1)
                            if g == AT_ADD:
                                add_totals(pn, pf)
                            if g == AT_INVERT:
                                invert(pn, pf)
                            if g == AT_NORM:
                                normalise(pn, pf, first)
                        if VS[i]:
                            v.wait_ge(expd, n * N2 + i + 1)
                        if g == 0 and not first:
                            v.wait_ge(den_ps, 2 * n + f - 1)
                        done = sum(VS[f * NG:i])
                        for k, (b, m, j, new) in enumerate(adds(g)):
                            src = Pb[:, slots[i], b:b + m]
                            if new:
                                v.tensor_copy(sums[:, f, j:j + m], src).then_inc(v_sum, 1)
                            else:
                                v.wait_ge(v_sum, n * 2 * VH + f * VH + AFTER[done + k])
                                v.tensor_tensor(sums[:, f, j:j + m], sums[:, f, j:j + m], src, ALU.add).then_inc(v_sum, 1)

                chunk(0, first=True)
                with v.Fori(1, NW) as n:
                    chunk(n)
                add_totals(NW - 1, 1)
                invert(NW - 1, 1)
                normalise(NW - 1, 1)
                v.wait_ge(x1_ready, 2 * (NW - 1))
                for t in range((NW - 1) * TW):
                    v.bn_stats(st[:, t], X1[:, t, :]).then_inc(stat, 1)
                for t in range((NW - 1) * TW):
                    v.wait_ge(stat, t + 1)
                    v.bn_aggr(mv[:, t, :], st[:, t]).then_inc(stat, 1)


def phase_c(nc, sb, sem, ps, ident, rwt, X1, st, mv, w1, w2, w3, normed, expert_out, out_v):
    with ExitStack() as c:
        gate = sb("gate", [P, 2, NT], F32, c)
        source = sb("source", [P, NA], I32, c)
        target = sb("target", [P, NA], I32, c)
        expert = sb("expert", [1, NTS], I32, c)
        WX = sb("WX", [P, 2 * E + AHEAD, CK, H], F32, c)
        WS = WX[:].rearrange("p m k h -> p (m k h)").bitcast(F16).rearrange("p (m a k h) -> p m a k h", a=2, k=CK, h=H)
        unscale = sb("unscale", [P, 1], F32, c)
        W2 = sb("W2", [P, E, HC, C], F32, c)
        route(nc, sb, sem, ps, ident, rwt, X1, st, mv, gate, source, target, expert, WX, WS, unscale, W2, w1, w2, w3, normed)
        experts(nc, sb, sem, ps, ident, source, target, expert, WS, unscale, W2, normed, expert_out)
        combine(nc, sb, sem, ps, ident, X1, gate, expert_out, out_v)


def route(nc, sb, sem, ps, ident, rwt, X1, st, mv, gate, source, target, expert, WX, WS, unscale, W2, w1, w2, w3, normed):
    with ExitStack() as c:
        XR = 16
        XH = sb("XH", [P, XR, C], F32, c)
        big = sb("big", [P, 2 * E, 1], F32, c)
        bound = sb("bound", [P, 1], F32, c)
        power = sb("power", [P, 4], F32, c)
        wscale = sb("wscale", [P, 1], F32, c)
        rs = sb("rs", [P, NT, 1], F32, c)
        XB = 3
        xt = sb("xt", [P, XB, CK, P], F32, c)
        lg = sb("lg", [P, NT, E], F32, c)
        pr = sb("pr", [P, NT, E], F32, c)
        best = sb("best", [P, NT, 1], F32, c)
        best2 = sb("best2", [P, NT, 1], F32, c)
        top = sb("top", [P, NT, 1], F32, c)
        rev = sb("rev", [P, E], F32, c)
        revi = sb("revi", [P, E], I32, c)
        ended = sb("ended", [1, NTS], F32, c)
        tmp = lg
        oh = [sb(f"oh{i}", [P, NT, E], F32, c) for i in range(2)]
        cnt = [pr, tmp]
        before = sb("before", [P, P], F32, c)
        ones = sb("ones_c", [P, P], F32, c)
        tiles_f = sb("tiles_f", [P, 3, E], F32, c)
        tiles_i = sb("tiles_i", [P, E], I32, c)
        epst = sb("epst", [P, 1], F32, c)
        count_i = xt[:, 0, 0].bitcast(I32)
        count = xt[:, 0, 1]
        spare_i = xt[:, 1, 0].bitcast(I32)
        spare = xt[:, 1, 1]
        RING = XR - 2
        small = XH[:, RING:XR].rearrange("p a c -> p (a c)").rearrange("p (n i t) -> p n i t", i=2, t=NT)
        number = small[:, 0]
        slot, slot_tile, slot_row = small[:, 1], small[:, 2], small[:, 3]
        number_i, slot_i, part_i = small[:, 4].bitcast(I32), small[:, 5].bitcast(I32), small[:, 6].bitcast(I32)
        w_in, cst, late, stat, aggr, var_r, std_r, xn, t_ps, t_cp, l_ps, ex, mx, ch, masks, ranks, hot, listed = [sem("r_" + n, c) for n in (
            "w_in", "cst", "late", "stat", "aggr", "var", "std", "xn", "t_ps", "t_cp", "l_ps", "ex", "mx", "ch", "masks", "ranks", "hot", "listed")]
        sized, bound_r, bound_ps, scaled, hi_r, lo_r = [sem("r_" + n, c) for n in ("sized", "bound_r", "bound_ps", "scaled", "hi_r", "lo_r")]
        x_out = [sem(f"r_x_out{i}", c) for i in range(4)]
        wx_in = [sem(f"r_wx_in{m}", c) for m in range(2 * E)]
        B3 = [P, NT, E]
        TP, LG, RK, TOT, LS, BND = (6, 7, 0), 3, 5, 4, 2, 1
        w1_v = w1.rearrange("(k p) e h -> p e k h", p=P)
        w3_v = w3.rearrange("(k p) e h -> p e k h", p=P)
        normed_v = normed.rearrange("(t p) c -> p t c", p=P)
        XO = 8
        with nc.Block() as block:
            @block.sync
            def _(sp):
                for e in range(E):
                    for m, w_v in ((2 * e, w1_v), (2 * e + 1, w3_v)):
                        sp.dma_start(WX[:, m + AHEAD], w_v[:, e]).then_inc(wx_in[m], 16)
                    if e in (E // 2 - 1, E - 1):
                        for i in (0, 1) if e < E - 1 else (2, 3):
                            sp.wait_ge(xn, (i + 1) * XO)
                            sp.dma_start(normed_v[:, i * XO:(i + 1) * XO], XH[:, i * XO % XR:i * XO % XR + XO]).then_inc(x_out[i], 16)
                for e in range(E):
                    sp.dma_start(W2[:, e, 0:HC - 1, :], w2[e, 0:(HC - 1) * P, :].rearrange("(k p) c -> p k c", p=P)).then_inc(w_in, 16)
                    sp.dma_start(W2[0:HL, e, HC - 1, :], w2[e, (HC - 1) * P:H, :]).then_inc(w_in, 16)
                sp.wait_ge(w_in, 16 * 2 * E)

            @block.gpsimd
            def _(g):
                g.iota(revi[:], pattern=[[-1, E]], base=E, channel_multiplier=0).then_inc(cst, 1)
                g.memset(epst[:], EPS_T).then_inc(cst, 1)
                g.memset(ones[:], 1.0).then_inc(cst, 1)
                g.memset(before[:], 0.0).then_inc(cst, 1)
                g.wait_ge(cst, 4)
                g.affine_select(out=before[:], in_=before[:], compare_op=ALU.is_ge, fill=1.0, base=0,
                                pattern=[[-1, P]], channel_multiplier=1).then_inc(cst, 1)
                g.wait_ge(cst, 5)
                g.wait_ge(l_ps, NT)
                g.iota(count_i, pattern=[[1, P]], base=0, channel_multiplier=0).then_inc(late, 1)
                for i in range(NT // XO):
                    g.wait_ge(x_out[i], 16)
                g.iota(number_i, pattern=[[S, 2], [P, NT]], base=1, channel_multiplier=1).then_inc(late, 1)
                g.iota(spare_i, pattern=[[P, P]], base=1 + 2 * S, channel_multiplier=1).then_inc(late, 1)
                for m in range(2 * E):
                    g.wait_ge(hi_r, 2 * (m + 1))
                    g.tensor_tensor(WS[:, m, LO], WX[:, m + AHEAD], WS[:, m, HI], ALU.subtract).then_inc(lo_r, 1)
                g.wait_ge(lo_r, 2 * E)

            @block.vector
            def _(v):
                n_ch = [0]

                def chain(ins):
                    n_ch[0] += 1
                    ins.then_inc(ch, 1)
                    v.wait_ge(ch, n_ch[0])

                for t in range(NT - TW, NT):
                    v.bn_stats(st[:, t], X1[:, t, :]).then_inc(stat, 1)
                for m in range(TW):
                    v.wait_ge(stat, m + 1)
                    v.bn_aggr(mv[:, NT - TW + m, :], st[:, NT - TW + m]).then_inc(aggr, 1)
                v.wait_ge(aggr, TW)
                v.tensor_copy(best[:, :, 0], mv[:, :, 0]).then_inc(var_r, 1)
                v.wait_ge(std_r, 1)
                chain(v.reciprocal(rs[:], rs[:]))
                v.wait_ge(var_r, 1)
                for t in range(NT):
                    if t >= XR:
                        v.wait_ge(t_ps, t - XR + 1)
                        v.wait_ge(x_out[(t - XR) // XO], 16)
                    v.tensor_scalar(XH[:, t % XR], X1[:, t], best[:, t], rs[:, t], ALU.subtract, ALU.mult).then_inc(xn, 1)
                def size(m):
                    v.wait_ge(wx_in[m], 16)
                    v.tensor_reduce(big[:, m], WX[:, m + AHEAD].rearrange("p k h -> p (k h)"), X, ALU.max, apply_absolute_value=True).then_inc(sized, 1)

                for m in range(2 * E):
                    size(m)
                v.wait_ge(sized, 2 * E)
                v.tensor_reduce(bound[:], big[:, :, 0], X, ALU.max).then_inc(bound_r, 1)
                v.wait_ge(bound_ps, 1)
                chain(v.tensor_scalar(bound[:], ps[:, BND, 0:1], 1e-30, None, ALU.max))
                bits = [power[:, i:i + 1] for i in range(4)]
                chain(v.tensor_scalar(bits[0].bitcast(I32), bound[:].bitcast(I32), 0x7f800000, None, ALU.bitwise_and))
                chain(v.tensor_copy(bits[1], bits[0].bitcast(I32)))
                chain(v.tensor_scalar(bits[2], bits[1], -1.0, float((2 * 127 + 13) * 2 ** 23), ALU.mult, ALU.add))
                v.tensor_copy(wscale[:].bitcast(I32), bits[2]).then_inc(scaled, 1)
                chain(v.tensor_scalar(bits[3], bits[1], float((13 + 4) * 2 ** 23), None, ALU.subtract))
                v.tensor_copy(unscale[:].bitcast(I32), bits[3]).then_inc(aggr, 1)
                v.wait_ge(l_ps, NT)
                chain(v.tensor_copy(lg[:], ps[:, LG, 0:NT * E].rearrange("p (t e) -> p t e", t=NT)))
                chain(v.tensor_reduce(best[:, :, 0], lg[:], X, ALU.max))
                v.tensor_tensor(lg[:], lg[:], best[:].broadcast_to(B3), ALU.subtract).then_inc(mx, 1)
                v.wait_ge(ex, 1)
                chain(v.tensor_reduce(best[:, :, 0], pr[:], X, ALU.add))
                chain(v.reciprocal(best[:], best[:]))
                chain(v.tensor_tensor(pr[:], pr[:], best[:].broadcast_to(B3), ALU.mult))
                v.wait_ge(cst, 5)
                chain(v.tensor_copy(rev[:], revi[:]))
                rev_b = rev[:].rearrange("p (a e) -> p a e", a=1).broadcast_to(B3)

                def pick(val, mask, probs):
                    chain(v.tensor_reduce(val[:, :, 0], probs[:], X, ALU.max))
                    chain(v.tensor_tensor(mask[:], probs[:], val[:].broadcast_to(B3), ALU.is_equal))
                    chain(v.tensor_tensor(mask[:], mask[:], rev_b, ALU.mult))
                    chain(v.tensor_reduce(top[:, :, 0], mask[:], X, ALU.max))
                    chain(v.tensor_tensor(mask[:], mask[:], top[:].broadcast_to(B3), ALU.is_equal))

                pick(best, oh[0], pr)
                chain(v.tensor_scalar(tmp[:], oh[0][:], -1.0, 1.0, ALU.mult, ALU.add))
                chain(v.tensor_tensor(tmp[:], tmp[:], pr[:], ALU.mult))
                chain(v.tensor_tensor(tmp[:], tmp[:], oh[0][:], ALU.subtract))
                pick(best2, oh[1], tmp)
                v.tensor_tensor(tmp[:], oh[0][:], oh[1][:], ALU.add).then_inc(masks, 1)
                chain(v.tensor_tensor(top[:], best[:], best2[:], ALU.add))
                chain(v.tensor_scalar(top[:], top[:], 1e-9, None, ALU.add))
                chain(v.reciprocal(top[:], top[:]))
                v.tensor_tensor(gate[:, 0], best[:, :, 0], top[:, :, 0], ALU.mult).then_inc(aggr, 1)
                v.tensor_tensor(gate[:, 1], best2[:, :, 0], top[:, :, 0], ALU.mult).then_inc(aggr, 1)
                v.wait_ge(late, 3)
                v.tensor_copy(number, number_i).then_inc(aggr, 1)
                v.tensor_copy(spare, spare_i).then_inc(aggr, 1)
                chain(v.tensor_copy(count, count_i))
                v.wait_ge(ranks, 1)
                tot = ps[:, TOT, 0:NT * E].rearrange("p (t e) -> p t e", t=NT)
                chain(v.tensor_copy(cnt[0][:], tot))
                cur, d = 0, 1
                while d < NT:
                    a, b = cnt[cur], cnt[1 - cur]
                    chain(v.tensor_copy(b[:, 0:d], a[:, 0:d]))
                    chain(v.tensor_tensor(b[:, d:NT], a[:, d:NT], a[:, 0:NT - d], ALU.add))
                    cur, d = 1 - cur, 2 * d
                total = cnt[cur]
                chain(v.tensor_scalar(tiles_f[:, 0], total[:, NT - 1], float(P - 1), None, ALU.add))
                chain(v.tensor_copy(tiles_i[:], tiles_f[:, 0]))
                chain(v.tensor_scalar(tiles_i[:], tiles_i[:], P.bit_length() - 1, None, ALU.logical_shift_right))
                chain(v.tensor_copy(tiles_f[:, 0], tiles_i[:]))
                src, d = 0, 1
                while d < E:
                    chain(v.tensor_copy(tiles_f[:, 1 - src, 0:d], tiles_f[:, src, 0:d]))
                    chain(v.tensor_tensor(tiles_f[:, 1 - src, d:E], tiles_f[:, src, d:E], tiles_f[:, src, 0:E - d], ALU.add))
                    src, d = 1 - src, 2 * d
                ends, base = tiles_f[:, src], tiles_f[:, 1 - src]
                chain(v.memset(ended[:], 0.0))
                for e in range(E):
                    chain(v.scalar_tensor_tensor(ended[:], count[0:1, 0:NTS], ends[0:1, e:e + 1], ended[:], ALU.is_ge, ALU.add))
                v.tensor_scalar(expert[:], ended[:], float(E - 1), None, ALU.min).then_inc(aggr, 1)
                chain(v.tensor_copy(tiles_f[:, 2], tiles_i[:]))
                chain(v.tensor_tensor(base, ends, tiles_f[:, 2], ALU.subtract))
                chain(v.tensor_scalar(base, base, float(P), None, ALU.mult))
                other = cnt[1 - cur]
                chain(v.tensor_tensor(other[:], total[:], tot, ALU.subtract))
                chain(v.tensor_tensor(other[:], other[:], ps[:, RK, 0:NT * E].rearrange("p (t e) -> p t e", t=NT), ALU.add))
                chain(v.tensor_tensor(other[:], other[:], base.rearrange("p (a e) -> p a e", a=1).broadcast_to(B3), ALU.add))
                for i in range(2):
                    chain(v.tensor_tensor(oh[i][:], oh[i][:], other[:], ALU.mult))
                    chain(v.tensor_reduce(best[:, :, 0], oh[i][:], X, ALU.add))
                    chain(v.tensor_copy(slot[:, i], best[:, :, 0]))
                chain(v.tensor_copy(slot_i, slot))
                chain(v.tensor_scalar(part_i, slot_i, P.bit_length() - 1, None, ALU.logical_shift_right))
                chain(v.tensor_copy(slot_tile, part_i))
                chain(v.tensor_scalar(part_i, slot_i, P - 1, None, ALU.bitwise_and))
                chain(v.tensor_copy(slot_row, part_i))
                v.wait_ge(aggr, TW + 6)
                for t in range(NT):
                    for i in range(2):
                        j = 2 * t + i
                        if j >= RING:
                            v.wait_ge(listed, j - RING + 1)
                        v.tensor_scalar(XH[:, j % RING, 0:P], count, slot_row[:, i, t:t + 1], None, ALU.is_equal).then_inc(hot, 1)
                        v.tensor_scalar(XH[:, j % RING, P:P + NA], count[:, 0:NA], slot_tile[:, i, t:t + 1], number[:, i, t:t + 1], ALU.is_equal, ALU.mult).then_inc(hot, 1)
                v.wait_ge(listed, 2 * NT)
                held, row, token, token_i = ps[:, LS, 0:NA], count[:, 0:NA], spare[:, 0:NA], spare_i[:, 0:NA]
                chain(v.scalar_tensor_tensor(row, held, 0.0, spare[:, 0:NA], ALU.is_equal, ALU.mult))
                chain(v.tensor_tensor(row, row, held, ALU.add))
                v.tensor_copy(target[:], row).then_inc(aggr, 1)
                chain(v.tensor_scalar(token, held, float(S - 1), None, ALU.add))
                chain(v.tensor_copy(token_i, token))
                v.tensor_scalar(source[:], token_i, S - 1, None, ALU.bitwise_and).then_inc(aggr, 1)

            @block.scalar
            def _(s):
                s.wait_ge(cst, 2)
                s.wait_ge(aggr, TW)
                s.activation(rs[:, :, 0], mv[:, :, 1], ACT.Sqrt, bias=epst[:]).then_inc(std_r, 1)
                for t in range(NT):
                    s.wait_ge(t_ps, t + 1)
                    if t >= XB:
                        s.wait_ge(l_ps, t - XB + 1)
                    s.activation(xt[:, t % XB], ps[:, TP[t % XB], 0:C].rearrange("p (k m) -> p k m", k=CK), ACT.Copy).then_inc(t_cp, 1)
                s.wait_ge(mx, 1)
                s.activation(pr[:], lg[:], ACT.Exp).then_inc(ex, 1)
                s.wait_ge(scaled, 1)
                for m in range(2 * E):
                    if m >= AHEAD:
                        s.wait_ge(lo_r, m - AHEAD + 1)
                    s.activation(WS[:, m, HI], WX[:, m + AHEAD], ACT.Copy, scale=wscale[:]).then_inc(hi_r, 1)
                    s.activation(WX[:, m + AHEAD], WX[:, m + AHEAD], ACT.Copy, scale=wscale[:]).then_inc(hi_r, 1)

            @block.tensor
            def _(pe):
                def turn(t):
                    pe.wait_ge(xn, t + 1)
                    if t >= XB:
                        pe.wait_ge(t_cp, t - XB + 1)
                    for k in range(CK):
                        m = pe.transpose(ps[:, TP[t % XB], k * P:(k + 1) * P], XH[:, t % XR, k * P:(k + 1) * P], ident[:])
                    m.then_inc(t_ps, 1)

                for t in range(XB - 1):
                    turn(t)
                for t in range(NT):
                    if t + XB - 1 < NT:
                        turn(t + XB - 1)
                    pe.wait_ge(t_cp, t + 1)
                    for k in range(CK):
                        m = pe.matmul(ps[:, LG, t * E:(t + 1) * E], xt[:, t % XB, k], rwt[:, k], start=k == 0, stop=k == CK - 1)
                    m.then_inc(l_ps, 1)
                pe.wait_ge(cst, 5)
                pe.wait_ge(bound_r, 1)
                pe.matmul(ps[:, BND, 0:1], ones[:], bound[:], start=True, stop=True).then_inc(bound_ps, 1)
                pe.wait_ge(masks, 1)
                both = tmp[:].rearrange("p t e -> p (t e)")
                pe.matmul(ps[:, RK, 0:NT * E], before[:], both, start=True, stop=True)
                pe.matmul(ps[:, TOT, 0:NT * E], ones[:], both, start=True, stop=True).then_inc(ranks, 1)
                for j in range(2 * NT):
                    pe.wait_ge(hot, 2 * (j + 1))
                    pe.matmul(ps[:, LS, 0:NA], XH[:, j % RING, 0:P], XH[:, j % RING, P:P + NA], start=j == 0, stop=j == 2 * NT - 1).then_inc(listed, 1)


def experts(nc, sb, sem, ps, ident, source, target, expert, WS, unscale, W2, normed, expert_out):
    with ExitStack() as c:
        xs = sb("xs", [P, 2, C], F32, c)
        xt = sb("xt2", [P, 2, CK, P], F16, c)
        sg = sb("sg", [P, H], F32, c)
        hh = sb("hh", [P, H], F32, c)
        hT = sb("hT", [P, HC, P], F32, c)
        y = sb("y", [P, 2, C], F32, c)
        t_ps, t_hi, t_cp, h1_ps, h3_ps, sg_r, h_r, ht_ps, ht_cp, ht_cs, y_ps, y_cp = [sem("e_" + n, c) for n in (
            "t_ps", "t_hi", "t_cp", "h1_ps", "h3_ps", "sg_r", "h_r", "ht_ps", "ht_cp", "ht_cs", "y_ps", "y_cp")]
        x_in = [sem(f"e_x_in{b}", c) for b in range(2)]
        y_out = [sem(f"e_y_out{b}", c) for b in range(2)]
        A1, A3, AT, AY, AX = 0, 2, 4, 6, 7
        halves = [(0, W), (W, H)]
        rows = [P] * (HC - 1) + [HL]

        def fetch(g, i):
            g.indirect_dma_start(xs[:, i % 2], None, normed[:, :], bass.IndirectOffsetOnAxis(source[:, i:i + 1], 0)).then_inc(x_in[i % 2], 16)

        def store(g, i):
            g.wait_ge(y_cp, i + 1)
            g.indirect_dma_start(expert_out[:, :], bass.IndirectOffsetOnAxis(target[:, i:i + 1], 0), y[:, i % 2], None).then_inc(y_out[i % 2], 16)

        with nc.Block() as block:
            @block.gpsimd
            def _(g):
                fetch(g, 0)
                fetch(g, 1)
                for i in range(NTS):
                    if i + 2 < NA:
                        g.wait_ge(t_ps, i + 1)
                        fetch(g, i + 2)
                    if i:
                        store(g, i - 1)
                store(g, NTS - 1)
                for b in range(2):
                    g.wait_ge(y_out[b], 16 * ((NTS + 1 - b) // 2))
                    g.wait_ge(x_in[b], 16 * ((NA + 1 - b) // 2))

            @block.tensor
            def _(pe):
                def turn_x(b, loads):
                    pe.wait_ge(x_in[b], 16 * loads)
                    for k in range(CK):
                        m = pe.transpose(ps[:, AX, k * P:(k + 1) * P], xs[:, b, k * P:(k + 1) * P], ident[:])
                    m.then_inc(t_ps, 1)

                def expand(w, bank, e, done):
                    terms = [(k, px, pw) for k in range(CK) for px, pw in ((HI, HI), (LO, HI), (HI, LO))]
                    for n, (a, b) in enumerate(halves):
                        for i, (k, px, pw) in enumerate(terms):
                            m = pe.matmul(ps[:, bank + n, 0:b - a], xt[:, px, k], WS[:, bass.ds(2 * e + w, 1), pw, k, a:b].rearrange("p a h -> p (a h)"),
                                          start=i == 0, stop=i == len(terms) - 1)
                    m.then_inc(done, 1)

                def turn_h(i):
                    pe.wait_ge(h_r, 2 * (i + 1))
                    for k in range(HC):
                        m = pe.transpose(ps[0:rows[k], AT + k // 4, (k % 4) * P:(k % 4 + 1) * P], hh[:, k * P:k * P + rows[k]], ident[:])
                    m.then_inc(ht_ps, 1)

                def shrink(i, e):
                    pe.wait_ge(ht_cp, 2 * (i + 1))
                    pe.wait_ge(ht_cs, i + 1)
                    for k in range(HC):
                        m = pe.matmul(ps[:, AY, 0:C], hT[0:rows[k], k], W2[0:rows[k], bass.ds(e, 1), k, :].rearrange("p a c -> p (a c)"), start=k == 0, stop=k == HC - 1)
                    m.then_inc(y_ps, 1)

                def load_expert(i):
                    return pe.value_load(expert[0:1, bass.ds(i, 1)], min_val=0, max_val=E - 1)

                turn_x(0, 1)
                pe.wait_ge(t_cp, 1)
                e0 = load_expert(0)
                expand(0, A1, e0, h1_ps)
                expand(1, A3, e0, h3_ps)
                turn_x(1, 1)
                with pe.Fori(0, (NTS - 1) // 2) as m:
                    for b in range(2):
                        i = 2 * m + 1 + b
                        e = load_expert(i)
                        pe.wait_ge(t_cp, i + 1)
                        pe.wait_ge(sg_r, i)
                        expand(0, A1, e, h1_ps)
                        turn_h(i - 1)
                        expand(1, A3, e, h3_ps)
                        turn_x(b, m + 2)
                        shrink(i - 1, load_expert(i - 1))
                turn_h(NTS - 1)
                shrink(NTS - 1, load_expert(NTS - 1))

            @block.scalar
            def _(s):
                def silu(i):
                    s.wait_ge(h1_ps, i + 1)
                    for n, (a, b) in enumerate(halves):
                        m = s.activation(sg[:, a:b], ps[:, A1 + n, 0:b - a], ACT.Silu, scale=unscale[:])
                    m.then_inc(sg_r, 1)

                def turned(i):
                    s.wait_ge(ht_ps, i + 1)
                    s.activation(hT[:, 0:4], ps[:, AT].rearrange("p (k m) -> p k m", k=4), ACT.Copy).then_inc(ht_cs, 1)

                silu(0)
                with s.Fori(1, NTS) as i:
                    s.wait_ge(h_r, 2 * i)
                    silu(i)
                    turned(i - 1)
                turned(NTS - 1)

            @block.vector
            def _(v):
                def x_copy(i):
                    v.wait_ge(t_ps, i + 1)
                    turned_x = ps[:, AX, 0:C].rearrange("p (k m) -> p k m", k=CK)
                    v.tensor_scalar(xt[:, HI], turned_x, XSCALE, None, ALU.mult).then_inc(t_hi, 1)
                    v.wait_ge(t_hi, i + 1)
                    v.scalar_tensor_tensor(xt[:, LO], turned_x, XSCALE, xt[:, HI], ALU.mult, ALU.subtract).then_inc(t_cp, 1)

                def gated(i):
                    v.wait_ge(sg_r, i + 1)
                    v.wait_ge(h3_ps, i + 1)
                    for n, (a, b) in enumerate(halves):
                        v.scalar_tensor_tensor(hh[:, a:b], ps[:, A3 + n, 0:b - a], unscale[:], sg[:, a:b], ALU.mult, ALU.mult).then_inc(h_r, 1)

                def turned(i):
                    v.wait_ge(ht_ps, i + 1)
                    v.tensor_copy(hT[:, 4], ps[:, AT + 1, 0:P]).then_inc(ht_cp, 1)
                    v.tensor_copy(hT[0:HL, 5], ps[0:HL, AT + 1, P:2 * P]).then_inc(ht_cp, 1)

                def y_copy(i, b, stored):
                    v.wait_ge(y_ps, i + 1)
                    if stored is not None:
                        v.wait_ge(y_out[b], stored)
                    v.tensor_copy(y[:, b], ps[:, AY, 0:C]).then_inc(y_cp, 1)

                x_copy(0)
                gated(0)
                v.wait_ge(h3_ps, 1)
                x_copy(1)
                v.wait_ge(ht_ps, 1)
                turned(0)
                v.wait_ge(h3_ps, 2)
                gated(1)
                x_copy(2)
                y_copy(0, 0, None)
                turned(1)
                gated(2)
                x_copy(3)
                y_copy(1, 1, None)
                with v.Fori(1, (NTS - 1) // 2) as m:
                    for b in range(2):
                        i = 2 * m + 1 + b
                        turned(i - 1)
                        gated(i)
                        x_copy(i + 1)
                        y_copy(i - 1, b, 16 * m)
                turned(NTS - 1)
                y_copy(NTS - 1, (NTS - 1) % 2, 16 * ((NTS - 1) // 2))


def combine(nc, sb, sem, ps, ident, X1, gate, expert_out, out_v):
    NB = 3
    out_of = [expert_out[1 + i * S:1 + (i + 1) * S, :].rearrange("(t p) c -> p t c", p=P) for i in range(2)]
    with ExitStack() as c:
        Y = sb("Y", [P, NB, 2, TW, C], F32, c)
        fin = sb("fin", [P, 2, C], F32, c)
        fo = sb("fo", [P, 2, CK, P], F32, c)
        y_in = [sem(f"y_in{b}", c) for b in range(NB)]
        part, fin_r, o_ps, o_cp = [sem("f_" + n, c) for n in ("part", "fin_r", "o_ps", "o_cp")]
        o_out = [sem(f"o_out{b}", c) for b in range(2)]
        with nc.Block() as block:
            @block.gpsimd
            def _(g):
                for n in range(NW):
                    if n >= NB:
                        g.wait_ge(fin_r, (n - NB + 1) * TW)
                    for i in range(2):
                        g.dma_start(Y[:, n % NB, i], out_of[i][:, n * TW:(n + 1) * TW]).then_inc(y_in[n % NB], 16)

            @block.vector
            def _(v):
                for t in range(NT):
                    n, m = divmod(t, TW)
                    if m == 0:
                        v.wait_ge(y_in[n % NB], 32 * (n // NB + 1))
                    if t >= 2:
                        v.wait_ge(o_ps, t - 1)
                    v.scalar_tensor_tensor(fin[:, t % 2], Y[:, n % NB, 0, m], gate[:, 0, t:t + 1], X1[:, t], ALU.mult, ALU.add).then_inc(part, 1)
                    v.wait_ge(part, t + 1)
                    v.scalar_tensor_tensor(fin[:, t % 2], Y[:, n % NB, 1, m], gate[:, 1, t:t + 1], fin[:, t % 2], ALU.mult, ALU.add).then_inc(fin_r, 1)

            @block.tensor
            def _(pe):
                for t in range(NT):
                    pe.wait_ge(fin_r, t + 1)
                    if t >= 2:
                        pe.wait_ge(o_cp, t - 1)
                    for k in range(CK):
                        m = pe.transpose(ps[:, t % 2, k * P:(k + 1) * P], fin[:, t % 2, k * P:(k + 1) * P], ident[:])
                    m.then_inc(o_ps, 1)

            @block.scalar
            def _(s):
                for t in range(NT):
                    s.wait_ge(o_ps, t + 1)
                    if t >= 2:
                        s.wait_ge(o_out[t % 2], 16 * (t // 2))
                    s.activation(fo[:, t % 2], ps[:, t % 2, 0:C].rearrange("p (k m) -> p k m", k=CK), ACT.Copy).then_inc(o_cp, 1)

            @block.sync
            def _(sp):
                for t in range(NT):
                    sp.wait_ge(o_cp, t + 1)
                    sp.dma_start(out_v[:, :, t * P:(t + 1) * P], fo[:, t % 2]).then_inc(o_out[t % 2], 16)
                for b in range(2):
                    sp.wait_ge(o_out[b], 16 * (NT // 2))


def kernel(**inputs):
    import numpy as np
    import concourse.bacc as bacc
    from concourse.bass_utils import run_bass_kernel_spmd

    laid = {
        "x": inputs["x"],
        "wqkv": np.transpose(inputs["L0_conv_w_qkv"]),
        "wproj": np.transpose(inputs["L0_conv_w_proj"]),
        "temp": inputs["L0_conv_temperature"],
        "rw": np.transpose(inputs["L0_ffn_router_w"]),
        "w1": np.transpose(inputs["L0_ffn_w1"], (2, 0, 1)),
        "w2": np.transpose(inputs["L0_ffn_w2"], (0, 2, 1)),
        "w3": np.transpose(inputs["L0_ffn_w3"], (2, 0, 1)),
    }
    nc = bacc.Bacc("TRN2", target_bir_lowering=False, num_devices=1)
    arrays, args = {}, []
    for name, a in laid.items():
        a = np.ascontiguousarray(a)
        arrays[f"in_{name}"] = a
        args.append(nc.dram_tensor(f"in_{name}", a.shape, mybir.dt.from_np(a.dtype), kind="ExternalInput").ap())
    args.append(nc.dram_tensor("result", (1, C, 64, 64), F32, kind="ExternalOutput").ap())
    build(nc, *args)
    r = run_bass_kernel_spmd(nc, [arrays], core_ids=[0])
    return r.results[0]["result"]
```
